# Optimizing a Trainium2 kernel written in Bass

```python
import numpy as np
import jax
import jax.numpy as jnp

def _softmax(x, axis=-1):
    return jax.nn.softmax(x, axis=axis)

def _gelu(x):
    return jax.nn.gelu(x, approximate=True)

def _silu(x):
    return jax.nn.silu(x)

def _sigmoid(x):
    return jax.nn.sigmoid(x)

def _layernorm(x, axis=-1, eps=1e-05):
    m = jnp.mean(x, axis=axis, keepdims=True)
    v = jnp.var(x, axis=axis, keepdims=True)
    return (x - m) / jnp.sqrt(v + eps)

def _scatter_add(tgt, idx, src, axis=0):
    return tgt.at[idx].add(src)

def _segment_sum(src, seg, n):
    return jax.ops.segment_sum(src, seg, n)
kernel_name = 'mk_dlrm_tower_d1_rec_r8_c82fa5'

def setup_inputs(seed: int=0):
    np.random.seed(seed)
    _w = jnp.asarray

    def _rec_inputs():
        import jax
        import jax.numpy as jnp
        _tk = jax.random.key(seed)
        dense_ctx = jax.random.normal(jax.random.fold_in(_tk, 190), (2048, 16), jnp.float32)
        ids = jnp.stack([jax.random.randint(jax.random.fold_in(_tk, 200 + f), (2048,), 0, v, jnp.int32) for f, v in enumerate([1000, 125000, 1250, 1250, 1250, 125000, 1000, 12500, 1250, 12500, 1000, 12500, 1000, 12500, 1000, 125000, 12500, 1000, 12500, 1250, 1250, 1250, 1000, 1000, 1000, 12500, 12500, 1000, 1250, 1000, 1250, 1000])], axis=1)
        tbl_0 = 0.05 * jax.random.normal(jax.random.fold_in(_tk, 500 + 0), (1000, 64), jnp.float32)
        tbl_1 = 0.05 * jax.random.normal(jax.random.fold_in(_tk, 500 + 1), (125000, 64), jnp.float32)
        tbl_2 = 0.05 * jax.random.normal(jax.random.fold_in(_tk, 500 + 2), (1250, 64), jnp.float32)
        tbl_3 = 0.05 * jax.random.normal(jax.random.fold_in(_tk, 500 + 3), (1250, 64), jnp.float32)
        tbl_4 = 0.05 * jax.random.normal(jax.random.fold_in(_tk, 500 + 4), (1250, 64), jnp.float32)
        tbl_5 = 0.05 * jax.random.normal(jax.random.fold_in(_tk, 500 + 5), (125000, 64), jnp.float32)
        tbl_6 = 0.05 * jax.random.normal(jax.random.fold_in(_tk, 500 + 6), (1000, 64), jnp.float32)
        tbl_7 = 0.05 * jax.random.normal(jax.random.fold_in(_tk, 500 + 7), (12500, 64), jnp.float32)
        tbl_8 = 0.05 * jax.random.normal(jax.random.fold_in(_tk, 500 + 8), (1250, 64), jnp.float32)
        tbl_9 = 0.05 * jax.random.normal(jax.random.fold_in(_tk, 500 + 9), (12500, 64), jnp.float32)
        tbl_10 = 0.05 * jax.random.normal(jax.random.fold_in(_tk, 500 + 10), (1000, 64), jnp.float32)
        tbl_11 = 0.05 * jax.random.normal(jax.random.fold_in(_tk, 500 + 11), (12500, 64), jnp.float32)
        tbl_12 = 0.05 * jax.random.normal(jax.random.fold_in(_tk, 500 + 12), (1000, 64), jnp.float32)
        tbl_13 = 0.05 * jax.random.normal(jax.random.fold_in(_tk, 500 + 13), (12500, 64), jnp.float32)
        tbl_14 = 0.05 * jax.random.normal(jax.random.fold_in(_tk, 500 + 14), (1000, 64), jnp.float32)
        tbl_15 = 0.05 * jax.random.normal(jax.random.fold_in(_tk, 500 + 15), (125000, 64), jnp.float32)
        tbl_16 = 0.05 * jax.random.normal(jax.random.fold_in(_tk, 500 + 16), (12500, 64), jnp.float32)
        tbl_17 = 0.05 * jax.random.normal(jax.random.fold_in(_tk, 500 + 17), (1000, 64), jnp.float32)
        tbl_18 = 0.05 * jax.random.normal(jax.random.fold_in(_tk, 500 + 18), (12500, 64), jnp.float32)
        tbl_19 = 0.05 * jax.random.normal(jax.random.fold_in(_tk, 500 + 19), (1250, 64), jnp.float32)
        tbl_20 = 0.05 * jax.random.normal(jax.random.fold_in(_tk, 500 + 20), (1250, 64), jnp.float32)
        tbl_21 = 0.05 * jax.random.normal(jax.random.fold_in(_tk, 500 + 21), (1250, 64), jnp.float32)
        tbl_22 = 0.05 * jax.random.normal(jax.random.fold_in(_tk, 500 + 22), (1000, 64), jnp.float32)
        tbl_23 = 0.05 * jax.random.normal(jax.random.fold_in(_tk, 500 + 23), (1000, 64), jnp.float32)
        tbl_24 = 0.05 * jax.random.normal(jax.random.fold_in(_tk, 500 + 24), (1000, 64), jnp.float32)
        tbl_25 = 0.05 * jax.random.normal(jax.random.fold_in(_tk, 500 + 25), (12500, 64), jnp.float32)
        tbl_26 = 0.05 * jax.random.normal(jax.random.fold_in(_tk, 500 + 26), (12500, 64), jnp.float32)
        tbl_27 = 0.05 * jax.random.normal(jax.random.fold_in(_tk, 500 + 27), (1000, 64), jnp.float32)
        tbl_28 = 0.05 * jax.random.normal(jax.random.fold_in(_tk, 500 + 28), (1250, 64), jnp.float32)
        tbl_29 = 0.05 * jax.random.normal(jax.random.fold_in(_tk, 500 + 29), (1000, 64), jnp.float32)
        tbl_30 = 0.05 * jax.random.normal(jax.random.fold_in(_tk, 500 + 30), (1250, 64), jnp.float32)
        tbl_31 = 0.05 * jax.random.normal(jax.random.fold_in(_tk, 500 + 31), (1000, 64), jnp.float32)
        _rk = jax.random.fold_in(_tk, 7)
        W_top1 = 0.0441942 * jax.random.normal(jax.random.fold_in(_tk, 801), (512, 512), jnp.float32)
        W_top2 = 0.0441942 * jax.random.normal(jax.random.fold_in(_tk, 802), (512, 256), jnp.float32)
        W_top3 = 0.0625 * jax.random.normal(jax.random.fold_in(_tk, 803), (256, 1), jnp.float32)
        b_top1 = jnp.zeros((512,), jnp.float32)
        b_top2 = jnp.zeros((256,), jnp.float32)
        return (dense_ctx, ids, tbl_0, tbl_1, tbl_2, tbl_3, tbl_4, tbl_5, tbl_6, tbl_7, tbl_8, tbl_9, tbl_10, tbl_11, tbl_12, tbl_13, tbl_14, tbl_15, tbl_16, tbl_17, tbl_18, tbl_19, tbl_20, tbl_21, tbl_22, tbl_23, tbl_24, tbl_25, tbl_26, tbl_27, tbl_28, tbl_29, tbl_30, tbl_31, W_top1, b_top1, W_top2, b_top2, W_top3)
    dense_ctx, ids, tbl_0, tbl_1, tbl_2, tbl_3, tbl_4, tbl_5, tbl_6, tbl_7, tbl_8, tbl_9, tbl_10, tbl_11, tbl_12, tbl_13, tbl_14, tbl_15, tbl_16, tbl_17, tbl_18, tbl_19, tbl_20, tbl_21, tbl_22, tbl_23, tbl_24, tbl_25, tbl_26, tbl_27, tbl_28, tbl_29, tbl_30, tbl_31, W_top1, b_top1, W_top2, b_top2, W_top3 = _rec_inputs()

    def _L0_rec_setup():
        import jax, jax.numpy as jnp
        import numpy as np
        NUM_FIELDS = 32
        BATCH = 2048
        EMBED_DIM = 64
        _pairs = np.array([(i, j) for i in range(NUM_FIELDS - 1) for j in range(i + 1, NUM_FIELDS)], dtype=np.int32)
        ROW = jnp.asarray(_pairs[:, 0])
        COL = jnp.asarray(_pairs[:, 1])
        key = jax.random.key(seed)
        x = jax.random.normal(key, (BATCH, NUM_FIELDS, EMBED_DIM), dtype=jnp.float32)
        return {'x': x}
    _L0_rec_all = _L0_rec_setup()
    _L0_rec_in = {k: v for k, v in _L0_rec_all.items() if k in ()}
    del _L0_rec_all
    return {'dense_ctx': dense_ctx, 'ids': ids, 'tbl_0': tbl_0, 'tbl_1': tbl_1, 'tbl_2': tbl_2, 'tbl_3': tbl_3, 'tbl_4': tbl_4, 'tbl_5': tbl_5, 'tbl_6': tbl_6, 'tbl_7': tbl_7, 'tbl_8': tbl_8, 'tbl_9': tbl_9, 'tbl_10': tbl_10, 'tbl_11': tbl_11, 'tbl_12': tbl_12, 'tbl_13': tbl_13, 'tbl_14': tbl_14, 'tbl_15': tbl_15, 'tbl_16': tbl_16, 'tbl_17': tbl_17, 'tbl_18': tbl_18, 'tbl_19': tbl_19, 'tbl_20': tbl_20, 'tbl_21': tbl_21, 'tbl_22': tbl_22, 'tbl_23': tbl_23, 'tbl_24': tbl_24, 'tbl_25': tbl_25, 'tbl_26': tbl_26, 'tbl_27': tbl_27, 'tbl_28': tbl_28, 'tbl_29': tbl_29, 'tbl_30': tbl_30, 'tbl_31': tbl_31, 'W_top1': W_top1, 'b_top1': b_top1, 'W_top2': W_top2, 'b_top2': b_top2, 'W_top3': W_top3}

def reference(dense_ctx, ids, tbl_0, tbl_1, tbl_2, tbl_3, tbl_4, tbl_5, tbl_6, tbl_7, tbl_8, tbl_9, tbl_10, tbl_11, tbl_12, tbl_13, tbl_14, tbl_15, tbl_16, tbl_17, tbl_18, tbl_19, tbl_20, tbl_21, tbl_22, tbl_23, tbl_24, tbl_25, tbl_26, tbl_27, tbl_28, tbl_29, tbl_30, tbl_31, W_top1, b_top1, W_top2, b_top2, W_top3):
    import jax
    import jax.numpy as jnp

    def _L0_rec_ref(x):
        import jax, jax.numpy as jnp
        import numpy as np
        NUM_FIELDS = 32
        BATCH = 2048
        EMBED_DIM = 64
        _pairs = np.array([(i, j) for i in range(NUM_FIELDS - 1) for j in range(i + 1, NUM_FIELDS)], dtype=np.int32)
        ROW = jnp.asarray(_pairs[:, 0])
        COL = jnp.asarray(_pairs[:, 1])
        s = jnp.sum(x, axis=-1)
        return s[:, ROW] * s[:, COL]
    e = jnp.stack([tbl_0[ids[:, 0]], tbl_1[ids[:, 1]], tbl_2[ids[:, 2]], tbl_3[ids[:, 3]], tbl_4[ids[:, 4]], tbl_5[ids[:, 5]], tbl_6[ids[:, 6]], tbl_7[ids[:, 7]], tbl_8[ids[:, 8]], tbl_9[ids[:, 9]], tbl_10[ids[:, 10]], tbl_11[ids[:, 11]], tbl_12[ids[:, 12]], tbl_13[ids[:, 13]], tbl_14[ids[:, 14]], tbl_15[ids[:, 15]], tbl_16[ids[:, 16]], tbl_17[ids[:, 17]], tbl_18[ids[:, 18]], tbl_19[ids[:, 19]], tbl_20[ids[:, 20]], tbl_21[ids[:, 21]], tbl_22[ids[:, 22]], tbl_23[ids[:, 23]], tbl_24[ids[:, 24]], tbl_25[ids[:, 25]], tbl_26[ids[:, 26]], tbl_27[ids[:, 27]], tbl_28[ids[:, 28]], tbl_29[ids[:, 29]], tbl_30[ids[:, 30]], tbl_31[ids[:, 31]]], axis=1)
    z = _L0_rec_ref(e)
    z = z.reshape(z.shape[0], -1)
    h = jnp.concatenate([z, dense_ctx], axis=1)
    h = jnp.maximum(h @ W_top1 + b_top1, 0.0)
    h = jnp.maximum(h @ W_top2 + b_top2, 0.0)
    y = h @ W_top3
    return y

_drawn_inputs = setup_inputs


def setup_inputs(seed=0):
    import zlib

    import numpy as np

    out = dict(_drawn_inputs(seed))
    spreads = {'b_top1': (0.0, 0.1), 'b_top2': (0.0, 0.1)}
    factors = {}
    for name, (base, spread) in spreads.items():
        noise = np.random.default_rng([zlib.crc32(name.encode()), seed]).standard_normal(out[name].shape)
        drawn = base * np.exp(spread * noise) if base else spread * noise
        out[name] = jnp.asarray(drawn.astype(out[name].dtype))
    for name, factor in factors.items():
        out[name] = (out[name] * factor).astype(out[name].dtype)
    return out
```

```python
from contextlib import ExitStack

import concourse.bass as bass
from concourse import mybir

P = 128
BATCH = 2048
FIELDS = 32
EMBED = 64
DENSE = 16
PAIRS = FIELDS * (FIELDS - 1) // 2
H1 = 512
H2 = 256
TILES = BATCH // P
CHUNK = 512
CT = CHUNK // P
CHUNKS = BATCH // CHUNK
K1 = (PAIRS + DENSE) // P
K2 = H1 // P
K3 = H2 // P
HALF = FIELDS // 2
RING = HALF - 1

W1_AT = 0
W2_AT = W1_AT + K1 * H1
W3_AT = W2_AT + K2 * H2
B1_AT = W3_AT + K3
B2_AT = B1_AT + K2
ID_AT = B2_AT + K3
WEIGHT_COLS = ID_AT + P


def pair_order():
    return [(i, (i + d) % FIELDS) for d in range(1, HALF) for i in range(FIELDS)] + [
        (i, i + HALF) for i in range(HALF)]


def build_program(nc, ids, dense, weights, tables, out):
    f32 = mybir.dt.float32
    f32r = mybir.dt.float32r
    i32 = mybir.dt.int32
    ALU = mybir.AluOpType
    ACT = mybir.ActivationFunctionType
    AX = mybir.AxisListType

    with ExitStack() as stack:
        hold = stack.enter_context
        ids_sb = hold(nc.sbuf_tensor([P, TILES, FIELDS], i32))
        dense_sb = hold(nc.sbuf_tensor([P, TILES, DENSE], f32))
        w_sb = hold(nc.sbuf_tensor([P, WEIGHT_COLS], f32))
        w1_hi = hold(nc.sbuf_tensor([P, K1, H1], f32r))
        w1_lo = hold(nc.sbuf_tensor([P, K1, H1], f32r))
        rows = hold(nc.sbuf_tensor([P, 2, CT * FIELDS, EMBED], f32))
        sums = hold(nc.sbuf_tensor([P, 2, CT, FIELDS + HALF], f32))
        z = hold(nc.sbuf_tensor([P, 2, CT, PAIRS + DENSE], f32))
        zt_hi = hold(nc.sbuf_tensor([P, K1, CHUNK], f32r))
        zt_lo = hold(nc.sbuf_tensor([P, K1, CHUNK], f32r))
        h1 = hold(nc.sbuf_tensor([P, K2, CHUNK], f32))
        h2 = hold(nc.sbuf_tensor([P, K3, CHUNK], f32))
        y_sb = hold(nc.sbuf_tensor([1, P, TILES], f32))
        zt_ps = hold(nc.psum_tensor([P, 2, CHUNK], f32))
        h_ps = hold(nc.psum_tensor([P, 4, CHUNK], f32))
        y_ps = hold(nc.psum_tensor([P, CHUNK], f32))
        ids_loaded = hold(nc.semaphore())
        dense_loaded = hold(nc.semaphore())
        weights_loaded = hold(nc.semaphore())
        w1_hi_ready = hold(nc.semaphore())
        w1_lo_ready = hold(nc.semaphore())
        rows_gathered_0 = hold(nc.semaphore())
        rows_gathered_1 = hold(nc.semaphore())
        rows_summed = hold(nc.semaphore())
        sums_extended = hold(nc.semaphore())
        z_ready = hold(nc.semaphore())
        dense_placed = hold(nc.semaphore())
        z_transposed = hold(nc.semaphore())
        zt_hi_ready = hold(nc.semaphore())
        zt_lo_ready = hold(nc.semaphore())
        layer1_done = hold(nc.semaphore())
        h1_ready = hold(nc.semaphore())
        layer2_done = hold(nc.semaphore())
        h2_ready = hold(nc.semaphore())
        layer3_done = hold(nc.semaphore())
        y_ready = hold(nc.semaphore())
        y_stored = hold(nc.semaphore())
        block = hold(nc.Block())
        rows_gathered = [rows_gathered_0, rows_gathered_1]
        w1 = w_sb[:, W1_AT:W2_AT].rearrange("p (k m) -> p k m", k=K1)
        w2 = w_sb[:, W2_AT:W3_AT].rearrange("p (k m) -> p k m", k=K2)
        w3 = w_sb[:, W3_AT:B1_AT]
        b1 = w_sb[:, B1_AT:B2_AT]
        b2 = w_sb[:, B2_AT:ID_AT]
        identity = w_sb[:, ID_AT:ID_AT + P]

        @block.sync
        def _(sp):
            sp.dma_start(ids_sb[:], ids.rearrange("(p t) f -> p t f", p=P)).then_inc(ids_loaded, 16)
            sp.dma_start(dense_sb[:], dense.rearrange("(p t) f -> p t f", p=P)).then_inc(dense_loaded, 16)
            sp.dma_start(w_sb[:], weights).then_inc(weights_loaded, 16)
            sp.wait_ge(y_ready, CHUNKS)
            sp.dma_start(out.rearrange("b o -> o b"), y_sb[0:1].rearrange("o p t -> o (p t)")).then_inc(y_stored, 16)
            sp.wait_ge(y_stored, 16)

        @block.gpsimd
        def _(pool):
            pool.wait_ge(ids_loaded, 16)
            for c in range(CHUNKS):
                if c >= 2:
                    pool.wait_ge(rows_summed, c - 1)
                for t in range(CT):
                    for f in range(FIELDS):
                        pool.indirect_dma_start(
                            rows[:, c % 2, t * FIELDS + f, :], None, tables[f],
                            bass.IndirectOffsetOnAxis(ap=ids_sb[:, c * CT + t, f:f + 1], axis=0),
                        ).then_inc(rows_gathered[c % 2], 16)

        @block.vector
        def _(dve):
            dve.wait_ge(w1_hi_ready, 1)
            nc.vector.tensor_tensor(w1_lo[:], w1, w1_hi[:].bitcast(f32), op=ALU.subtract).then_inc(w1_lo_ready, 1)
            for c in range(CHUNKS):
                s = sums[:, c % 2]
                dve.wait_ge(rows_gathered[c % 2], 16 * CT * FIELDS * (c // 2 + 1))
                nc.vector.tensor_reduce(s[:, :, 0:FIELDS], rows[:, c % 2].rearrange("p (t f) e -> p t f e", t=CT),
                                        axis=AX.X, op=ALU.add).then_inc(rows_summed, 1)
                dve.wait_ge(rows_summed, c + 1)
                nc.vector.tensor_copy(s[:, :, FIELDS:FIELDS + HALF], s[:, :, 0:HALF]).then_inc(sums_extended, 1)
                dve.wait_ge(sums_extended, c + 1)
                if c >= 2:
                    dve.wait_ge(z_transposed, K1 * (c - 1))
                for t in range(CT):
                    first = s[:, t, None, 0:FIELDS].to_broadcast([P, RING, FIELDS])
                    v = s[:, t, 1:1 + RING]
                    second = bass.AP(tensor=v.tensor, offset=v.offset, ap=[list(v.ap[0]), [1, RING], [1, FIELDS]])
                    nc.vector.tensor_tensor(z[:, c % 2, t, 0:RING * FIELDS].rearrange("p (d i) -> p d i", d=RING),
                                            first, second, op=ALU.mult)
                nc.vector.tensor_tensor(z[:, c % 2, :, RING * FIELDS:PAIRS], s[:, :, 0:HALF], s[:, :, HALF:FIELDS],
                                        op=ALU.mult).then_inc(z_ready, 1)
                for k in range(K1):
                    n = c * K1 + k
                    dve.wait_ge(zt_hi_ready, n + 1)
                    nc.vector.tensor_tensor(zt_lo[:, k], zt_ps[:, n % 2], zt_hi[:, k].bitcast(f32),
                                            op=ALU.subtract).then_inc(zt_lo_ready, 1)

        @block.scalar
        def _(act):
            act.wait_ge(weights_loaded, 16)
            nc.scalar.copy(w1_hi[:], w1).then_inc(w1_hi_ready, 1)
            act.wait_ge(dense_loaded, 16)
            for c in range(CHUNKS):
                if c >= 2:
                    act.wait_ge(z_transposed, K1 * (c - 1))
                nc.scalar.copy(z[:, c % 2, :, PAIRS:], dense_sb[:, c * CT:(c + 1) * CT, :]).then_inc(dense_placed, 1)
                for k in range(K1):
                    n = c * K1 + k
                    if k == 0 and c:
                        act.wait_ge(layer1_done, K2 * c)
                    act.wait_ge(z_transposed, n + 1)
                    nc.scalar.copy(zt_hi[:, k], zt_ps[:, n % 2]).then_inc(zt_hi_ready, 1)
                for m in range(K2):
                    n = c * K2 + m
                    if m == 0 and c:
                        act.wait_ge(layer2_done, K3 * c)
                    act.wait_ge(layer1_done, n + 1)
                    nc.scalar.activation(h1[:, m], h_ps[:, n % 2], ACT.Relu, bias=b1[:, m:m + 1]).then_inc(h1_ready, 1)
                for m in range(K3):
                    n = c * K3 + m
                    if m == 0 and c:
                        act.wait_ge(layer3_done, c)
                    act.wait_ge(layer2_done, n + 1)
                    nc.scalar.activation(h2[:, m], h_ps[:, 2 + m], ACT.Relu, bias=b2[:, m:m + 1]).then_inc(h2_ready, 1)
                act.wait_ge(layer3_done, c + 1)
                nc.scalar.copy(y_sb[0:1, :, c * CT:(c + 1) * CT].rearrange("o p t -> o t p"),
                               y_ps[0:1, :].rearrange("o (t p) -> o t p", t=CT)).then_inc(y_ready, 1)

        @block.tensor
        def _(pe):
            pe.wait_ge(weights_loaded, 16)
            for c in range(CHUNKS):
                pe.wait_ge(z_ready, c + 1)
                pe.wait_ge(dense_placed, c + 1)
                for k in range(K1):
                    n = c * K1 + k
                    if n >= 2:
                        pe.wait_ge(zt_lo_ready, n - 1)
                    for t in range(CT):
                        last = nc.tensor.transpose(zt_ps[:, n % 2, t * P:(t + 1) * P],
                                                   z[:, c % 2, t, k * P:(k + 1) * P], identity)
                    last.then_inc(z_transposed, 1)
                if c == 0:
                    pe.wait_ge(w1_lo_ready, 1)
                for m in range(K2):
                    n = c * K2 + m
                    if n >= 2:
                        pe.wait_ge(h1_ready, n - 1)
                    for k in range(K1):
                        if m == 0:
                            pe.wait_ge(zt_lo_ready, c * K1 + k + 1)
                        w_hi, w_lo = (w[:, k, m * P:(m + 1) * P] for w in (w1_hi, w1_lo))
                        nc.tensor.matmul(h_ps[:, n % 2], w_hi, zt_hi[:, k], start=k == 0, stop=False)
                        nc.tensor.matmul(h_ps[:, n % 2], w_hi, zt_lo[:, k], start=False, stop=False)
                        last = nc.tensor.matmul(h_ps[:, n % 2], w_lo, zt_hi[:, k], start=False, stop=k == K1 - 1)
                    last.then_inc(layer1_done, 1)
                for m in range(K3):
                    if c:
                        pe.wait_ge(h2_ready, K3 * (c - 1) + m + 1)
                    for k in range(K2):
                        pe.wait_ge(h1_ready, c * K2 + k + 1)
                        last = nc.tensor.matmul(h_ps[:, 2 + m], w2[:, k, m * P:(m + 1) * P], h1[:, k],
                                                start=k == 0, stop=k == K2 - 1)
                    last.then_inc(layer2_done, 1)
                if c:
                    pe.wait_ge(y_ready, c)
                for k in range(K3):
                    pe.wait_ge(h2_ready, c * K3 + k + 1)
                    last = nc.tensor.matmul(y_ps[0:1, :], w3[:, k:k + 1], h2[:, k], start=k == 0, stop=k == K3 - 1)
                last.then_inc(layer3_done, 1)


def kernel(**inputs):
    import numpy as _np
    import concourse.bacc as _bacc
    from concourse import mybir as _mybir
    from concourse.bass_utils import run_bass_kernel_spmd as _run

    nc = _bacc.Bacc("TRN2", target_bir_lowering=False, num_devices=1)
    arrays = {}

    def put(name, a):
        arrays[name] = a = _np.ascontiguousarray(a)
        return nc.dram_tensor(name, a.shape, _mybir.dt.from_np(a.dtype), kind="ExternalInput").ap()

    row_of = {}
    for i in range(FIELDS - 1):
        for j in range(i + 1, FIELDS):
            row_of[i, j] = row_of[j, i] = len(row_of) // 2
    order = [row_of[p] for p in pair_order()] + list(range(PAIRS, PAIRS + DENSE))

    def by_partition(w):
        w = _np.asarray(w).reshape(-1, P, w.shape[-1] if w.ndim > 1 else 1)
        return w.transpose(1, 0, 2).reshape(P, -1)

    weights = _np.concatenate(
        [by_partition(_np.asarray(inputs["W_top1"])[order])]
        + [by_partition(inputs[n]) for n in ("W_top2", "W_top3", "b_top1", "b_top2")]
        + [_np.eye(P, dtype=_np.float32)], axis=1)
    args = [put("ids", inputs["ids"]), put("dense_ctx", inputs["dense_ctx"]), put("weights", weights),
            [put(f"tbl_{f}", inputs[f"tbl_{f}"]) for f in range(FIELDS)],
            nc.dram_tensor("out", (BATCH, 1), _mybir.dt.float32, kind="ExternalOutput").ap()]
    build_program(nc, *args)
    r = _run(nc, [arrays], core_ids=[0])
    return r.results[0]["out"]
```

```python
from contextlib import ExitStack

import concourse.bass as bass
from concourse import mybir

P = 128
BATCH = 2048
FIELDS = 32
EMBED = 64
DENSE = 16
PAIRS = FIELDS * (FIELDS - 1) // 2
H1 = 512
H2 = 256
TILES = BATCH // P
K1 = (PAIRS + DENSE) // P
K2 = H1 // P
K3 = H2 // P
HALF = FIELDS // 2
RING = HALF - 1

VOCAB = [1000, 125000, 1250, 1250, 1250, 125000, 1000, 12500, 1250, 12500, 1000, 12500, 1000, 12500, 1000, 125000,
         12500, 1000, 12500, 1250, 1250, 1250, 1000, 1000, 1000, 12500, 12500, 1000, 1250, 1000, 1250, 1000]
SLOTS = [f for v in (1000, 1250, 12500, 125000) for f in range(FIELDS) if VOCAB[f] == v]

CHUNK_TILES = [4, 4, 4, 2, 2]
CHUNK_SELECTED = [0, 5, 5, 5, 5]
CHUNKS = len(CHUNK_TILES)
FIRST_TILE = [sum(CHUNK_TILES[:c]) for c in range(CHUNKS)]
CT = max(CHUNK_TILES)
CHUNK = CT * P

A_SLOTS = VOCAB.count(1000)
B_SLOTS = VOCAB.count(1250)
SMALL = A_SLOTS + B_SLOTS
MIDDLE = VOCAB.count(12500)
M_SEL = max(CHUNK_SELECTED)
A_GROUPS = A_SLOTS // 2
B_GROUPS = (B_SLOTS + 1) // 2
S_GROUPS = A_GROUPS + B_GROUPS
SEL_SLOTS = SMALL + M_SEL
LA, LB, LM = 16, 20, 98
A_COLS = A_GROUPS * LA
B_COLS = B_GROUPS * LB
S_COLS = A_COLS + B_COLS
V_SMALL = 2 * S_COLS
RS_COLS = S_COLS + M_SEL * LM

SHIFT = 17
MULTIPLIER = {LA: 16384, LB: 13108, LM: 2675}
for _length, _rows in ((LA, 1000), (LB, 1250), (LM, 12500)):
    assert (_rows >> 1) * MULTIPLIER[_length] < 1 << 24
    assert all(((r >> 1) * MULTIPLIER[_length]) >> SHIFT == r // _length for r in range(_rows))

PIECES = [("a", 0, j * A_COLS // 2, A_COLS // 2) for j in range(2)]
PIECES += [("b", 0, j * B_COLS // 2, B_COLS // 2) for j in range(2)]
PIECES += [("m", m, j * LM // 2, LM // 2) for m in range(M_SEL) for j in range(2)]
PIECE_SLOTS = 3
PIECE_COLS = max(n for _, _, _, n in PIECES)
SMALL_PIECES = 4

W2_AT = 0
W3_AT = W2_AT + K2 * H2
B1_AT = W3_AT + K3
B2_AT = B1_AT + K2
ID_AT = B2_AT + K3
WEIGHT_COLS = ID_AT + P
GROUPS = S_GROUPS + M_SEL

BANKS = 3


def _hi(c):
    return [("hi", c, g) for g in range(S_GROUPS + CHUNK_SELECTED[c])]


def _mlp(c):
    return [("l1", c, m) for m in range(K2)] + [("l2", c, m) for m in range(K3)] + [("l3", c, 0)]


BANK_ORDER = _hi(0) + _hi(1) + _hi(2) + _mlp(0) + _hi(3) + _mlp(1) + _hi(4) + _mlp(2) + _mlp(3) + _mlp(4)
BANK_USE = {use: n for n, use in enumerate(BANK_ORDER)}


def _small(c):
    return [("small", c, t) for t in range(CHUNK_TILES[c])]


def _middle(c):
    return [("middle", c, t) for t in range(CHUNK_TILES[c] if CHUNK_SELECTED[c] else 0)]


CANDIDATE_ORDER = (_small(0) + _small(1) + _small(2) + _middle(1) + _small(3) + _middle(2) + _small(4) + _middle(3)
                   + _middle(4))
CANDIDATE_USE = {use: n for n, use in enumerate(CANDIDATE_ORDER)}
BETWEEN = [_small(2), _small(3) + _middle(2), _small(4) + _middle(3), _middle(4), []]


def pair_order():
    return [(i, (i + d) % FIELDS) for d in range(1, HALF) for i in range(FIELDS)] + [
        (i, i + HALF) for i in range(HALF)]


def build_program(nc, ids, ids_by_slot, dense, w1, weights, selectors, multipliers, rows_a, rows_b, rows_m, tables, out):
    f32 = mybir.dt.float32
    f32r = mybir.dt.float32r
    bf16 = mybir.dt.bfloat16
    i32 = mybir.dt.int32
    ALU = mybir.AluOpType
    ACT = mybir.ActivationFunctionType
    AX = mybir.AxisListType

    with ExitStack() as stack:
        hold = stack.enter_context
        ids_sb = hold(nc.sbuf_tensor([P, TILES, FIELDS], i32))
        hi_int = hold(nc.sbuf_tensor([P, TILES, SEL_SLOTS], i32))
        lo = hold(nc.sbuf_tensor([P, TILES, SEL_SLOTS], f32))
        hi_by_slot = hold(nc.sbuf_tensor([SEL_SLOTS, BATCH], bf16))
        selector = hold(nc.sbuf_tensor([SEL_SLOTS, GROUPS, P], bf16))
        multiplier = hold(nc.sbuf_tensor([SEL_SLOTS, 1], f32))
        pieces = hold(nc.sbuf_tensor([P, PIECE_SLOTS, PIECE_COLS, EMBED], f32))
        row_sums = hold(nc.sbuf_tensor([P, RS_COLS], f32))
        rest = hold(nc.sbuf_tensor([P, RS_COLS], f32))
        small_parts = hold(nc.sbuf_tensor([P, 3, V_SMALL], bf16))
        middle_parts = hold(nc.sbuf_tensor([P, 3, M_SEL * LM], bf16))
        small_hot = hold(nc.sbuf_tensor([P, 2, S_GROUPS, CHUNK], bf16))
        middle_hot = hold(nc.sbuf_tensor([P, 2, M_SEL, CHUNK], bf16))
        lo_hot = hold(nc.sbuf_tensor([P, CT, V_SMALL], bf16))
        picked = hold(nc.sbuf_tensor([P, CT, V_SMALL], f32))
        picked_middle = hold(nc.sbuf_tensor([P, 2, M_SEL, LM], bf16))
        lane64 = hold(nc.sbuf_tensor([P, 1], f32))
        lane128 = hold(nc.sbuf_tensor([P, 1], f32))
        count_small = hold(nc.sbuf_tensor([P, V_SMALL], bf16))
        count_middle = hold(nc.sbuf_tensor([P, LM], f32))
        gathered_even = hold(nc.sbuf_tensor([P, CT * (FIELDS - SMALL), EMBED], f32))
        gathered_odd = hold(nc.sbuf_tensor([P, CT * (FIELDS - SMALL - CHUNK_SELECTED[1]), EMBED], f32))
        sums = hold(nc.sbuf_tensor([P, 2, CT, FIELDS + HALF], f32))
        dense_sb = hold(nc.sbuf_tensor([P, TILES, DENSE], f32))
        w_sb = hold(nc.sbuf_tensor([P, WEIGHT_COLS], f32))
        w1_hi = hold(nc.sbuf_tensor([P, K1, H1], f32r))
        w1_lo = hold(nc.sbuf_tensor([P, K1, H1], f32r))
        z = hold(nc.sbuf_tensor([P, 2, CT, PAIRS + DENSE], f32))
        zt_hi = hold(nc.sbuf_tensor([P, K1, CHUNK], f32r))
        zt_lo = hold(nc.sbuf_tensor([P, K1, CHUNK], f32r))
        h1 = hold(nc.sbuf_tensor([P, K2, CHUNK], f32))
        h2 = hold(nc.sbuf_tensor([P, K3, CHUNK], f32))
        y_sb = hold(nc.sbuf_tensor([1, 2, CHUNK], f32))
        zt_ps = hold(nc.psum_tensor([P, 2, CHUNK], f32))
        bank_ps = hold(nc.psum_tensor([P, BANKS, CHUNK], f32))
        cand_ps = hold(nc.psum_tensor([P, 2, 512], f32))

        ids_loaded = hold(nc.semaphore("ids_loaded"))
        ids_by_slot_loaded = hold(nc.semaphore("ids_by_slot_loaded"))
        multipliers_loaded = hold(nc.semaphore("multipliers_loaded"))
        selectors_loaded = hold(nc.semaphore("selectors_loaded"))
        dense_loaded = hold(nc.semaphore("dense_loaded"))
        w1_loaded = hold(nc.semaphore("w1_loaded"))
        weights_loaded = hold(nc.semaphore("weights_loaded"))
        piece_loaded = [hold(nc.semaphore(f"piece_loaded_{s}")) for s in range(PIECE_SLOTS)]
        piece_summed = hold(nc.semaphore("piece_summed"))
        constants_ready = hold(nc.semaphore("constants_ready"))
        parts_cleared = hold(nc.semaphore("parts_cleared"))
        hi_steps = hold(nc.semaphore("hi_steps"))
        lo_steps = hold(nc.semaphore("lo_steps"))
        hi_ready = hold(nc.semaphore("hi_ready"))
        selector_ready = hold(nc.semaphore("selector_ready"))
        split_steps = hold(nc.semaphore("split_steps"))
        parts_ready = hold(nc.semaphore("parts_ready"))
        hot_ready = hold(nc.semaphore("hot_ready"))
        lo_hot_ready = hold(nc.semaphore("lo_hot_ready"))
        candidates_ready = hold(nc.semaphore("candidates_ready"))
        candidates_read = hold(nc.semaphore("candidates_read"))
        rows_gathered = [hold(nc.semaphore(f"rows_gathered_{c}")) for c in range(CHUNKS)]
        small_summed = hold(nc.semaphore("small_summed"))
        rows_summed = hold(nc.semaphore("rows_summed"))
        sums_extended = hold(nc.semaphore("sums_extended"))
        w1_hi_ready = hold(nc.semaphore("w1_hi_ready"))
        w1_lo_ready = hold(nc.semaphore("w1_lo_ready"))
        z_ready = hold(nc.semaphore("z_ready"))
        dense_placed = hold(nc.semaphore("dense_placed"))
        z_transposed = hold(nc.semaphore("z_transposed"))
        zt_hi_ready = hold(nc.semaphore("zt_hi_ready"))
        zt_lo_ready = hold(nc.semaphore("zt_lo_ready"))
        bank_filled = hold(nc.semaphore("bank_filled"))
        bank_read = hold(nc.semaphore("bank_read"))
        y_stored = [hold(nc.semaphore(f"y_stored_{s}")) for s in range(2)]
        block = hold(nc.Block())

        w2 = w_sb[:, W2_AT:W3_AT].rearrange("p (k m) -> p k m", k=K2)
        w3 = w_sb[:, W3_AT:B1_AT]
        b1 = w_sb[:, B1_AT:B2_AT]
        b2 = w_sb[:, B2_AT:ID_AT]
        identity = w_sb[:, ID_AT:ID_AT + P]
        slot_ids = z[0:SEL_SLOTS, 0].rearrange("p t k -> p (t k)").bitcast(i32)
        selectors_in = z[0:SEL_SLOTS, 1].rearrange("p t k -> p (t k)")

        def gathered(c):
            n = FIELDS - SMALL - CHUNK_SELECTED[c]
            buffer = (gathered_even, gathered_odd)[c % 2]
            return buffer[:, 0:CHUNK_TILES[c] * n, :].rearrange("p (t f) e -> p t f e", t=CHUNK_TILES[c])

        @block.sync
        def _(sp):
            def load_piece(n):
                kind, m, first, cols = PIECES[n]
                source = {"a": rows_a, "b": rows_b}[kind] if kind != "m" else rows_m[m]
                if n >= PIECE_SLOTS:
                    sp.wait_ge(piece_summed, n - PIECE_SLOTS + 1)
                sp.dma_start(pieces[:, n % PIECE_SLOTS, 0:cols, :].rearrange("p c e -> p (c e)"),
                             source[:, first * EMBED:(first + cols) * EMBED]).then_inc(piece_loaded[n % PIECE_SLOTS], 16)

            sp.dma_start(ids_sb[:], ids.rearrange("(p t) f -> p t f", p=P)).then_inc(ids_loaded, 16)
            sp.dma_start(slot_ids[:, 0:BATCH], ids_by_slot).then_inc(ids_by_slot_loaded, 16)
            load_piece(0)
            load_piece(1)
            load_piece(2)
            sp.dma_start(w_sb[:], weights).then_inc(weights_loaded, 16)
            sp.dma_start(h1[:].rearrange("p k m -> p (k m)"), w1).then_inc(w1_loaded, 16)
            sp.dma_start(dense_sb[:], dense.rearrange("(p t) f -> p t f", p=P)).then_inc(dense_loaded, 16)
            for n in range(3, len(PIECES)):
                load_piece(n)
            for c in range(CHUNKS):
                n = CHUNK_TILES[c] * P
                first = FIRST_TILE[c] * P
                sp.wait_ge(bank_read, BANK_USE["l3", c, 0] + 1)
                sp.dma_start(out[:, first:first + n], y_sb[0:1, c % 2, 0:n]).then_inc(y_stored[c % 2], 16)
            sp.wait_ge(y_stored[0], 16 * ((CHUNKS + 1) // 2))
            sp.wait_ge(y_stored[1], 16 * (CHUNKS // 2))

        @block.gpsimd
        def _(pool):
            for h in range(2):
                nc.gpsimd.iota(lane64[h * 64:h * 64 + 64, :], [[0, 1]], 0, 1,
                               allow_small_or_imprecise_dtypes=True).then_inc(constants_ready, 1)
            pool.wait_ge(constants_ready, 2)
            nc.gpsimd.iota(lane128[:], [[0, 1]], 0, 1, allow_small_or_imprecise_dtypes=True).then_inc(constants_ready, 1)
            nc.gpsimd.iota(count_small[:, 0:2 * A_COLS], [[0, 2 * A_GROUPS], [1, LA]], 0, 0,
                           allow_small_or_imprecise_dtypes=True).then_inc(constants_ready, 1)
            nc.gpsimd.iota(count_small[:, 2 * A_COLS:], [[0, 2 * B_GROUPS], [1, LB]], 0, 0,
                           allow_small_or_imprecise_dtypes=True).then_inc(constants_ready, 1)
            nc.gpsimd.iota(count_middle[:], [[1, LM]], 0, 0,
                           allow_small_or_imprecise_dtypes=True).then_inc(constants_ready, 1)
            pool.wait_ge(ids_loaded, 16)
            for c in range(CHUNKS):
                if c >= 2:
                    pool.wait_ge(rows_summed, c - 1)
                for t in range(CHUNK_TILES[c]):
                    for n, slot in enumerate(range(SMALL + CHUNK_SELECTED[c], FIELDS)):
                        pool.indirect_dma_start(
                            gathered(c)[:, t, n, :], None, tables[slot],
                            bass.IndirectOffsetOnAxis(ap=ids_sb[:, FIRST_TILE[c] + t, slot:slot + 1], axis=0),
                        ).then_inc(rows_gathered[c], 16)

        @block.vector
        def _(dve):
            def sum_piece(n):
                kind, m, first, cols = PIECES[n]
                at = {"a": 0, "b": A_COLS, "m": S_COLS + m * LM}[kind] + first
                dve.wait_ge(piece_loaded[n % PIECE_SLOTS], 16 * (n // PIECE_SLOTS + 1))
                nc.vector.tensor_reduce(row_sums[:, at:at + cols], pieces[:, n % PIECE_SLOTS, 0:cols, :],
                                        axis=AX.X, op=ALU.add).then_inc(piece_summed, 1)

            def split(regions, parts, step):
                for r in range(3):
                    source = row_sums if r == 0 else rest
                    for p0, p1, src, dst, n in regions:
                        nc.vector.tensor_copy(parts[p0:p1, r, dst:dst + n],
                                              source[p0:p1, src:src + n]).then_inc(split_steps, 1)
                    step += len(regions)
                    dve.wait_ge(split_steps, step)
                    if r < 2:
                        for p0, p1, src, dst, n in regions:
                            nc.vector.tensor_tensor(rest[p0:p1, src:src + n], source[p0:p1, src:src + n],
                                                    parts[p0:p1, r, dst:dst + n],
                                                    op=ALU.subtract).then_inc(split_steps, 1)
                        step += len(regions)
                        dve.wait_ge(split_steps, step)
                dve.sem_inc(parts_ready, 1)
                return step

            def make_hot(c):
                n = CHUNK_TILES[c] * P
                nt = CHUNK_TILES[c]
                t0 = FIRST_TILE[c]
                for h0, slots, groups, length in ((0, 0, A_SLOTS, LA), (2 * A_COLS, A_SLOTS, 2 * B_GROUPS, LB)):
                    nc.vector.tensor_tensor(
                        lo_hot[:, 0:nt, h0:h0 + groups * length].rearrange("p t (f l) -> p t f l", l=length),
                        count_small[:, None, h0:h0 + groups * length].to_broadcast(
                            [P, nt, groups * length]).rearrange("p t (f l) -> p t f l", l=length),
                        lo[:, t0:t0 + nt, slots:slots + groups, None].to_broadcast([P, nt, groups, length]),
                        op=ALU.is_equal).then_inc(lo_hot_ready, 1)
                last = BANK_USE[_hi(c)[-1]]
                dve.wait_ge(bank_read, last + 1)
                hot = small_hot[:, c % 2, :, 0:n]
                nc.vector.tensor_scalar(hot, hot, lane64[:], None, op0=ALU.is_equal).then_inc(hot_ready, 1)
                if CHUNK_SELECTED[c]:
                    hot = middle_hot[:, c % 2, 0:CHUNK_SELECTED[c], 0:n]
                    nc.vector.tensor_scalar(hot, hot, lane128[:], None, op0=ALU.is_equal).then_inc(hot_ready, 1)

            def pick_small(c):
                nt = CHUNK_TILES[c]
                s = sums[:, c % 2]
                dve.wait_ge(lo_hot_ready, 2 * c + 2)
                for t in range(nt):
                    n = CANDIDATE_USE["small", c, t]
                    dve.wait_ge(candidates_ready, n + 1)
                    nc.vector.tensor_tensor(picked[:, t], lo_hot[:, t], cand_ps[:, n % 2, 0:V_SMALL],
                                            op=ALU.mult).then_inc(candidates_read, 1)
                dve.wait_ge(candidates_read, CANDIDATE_USE["small", c, nt - 1] + 1)
                nc.vector.tensor_reduce(
                    s[:, 0:nt, 0:A_SLOTS],
                    picked[:, 0:nt, 0:2 * A_COLS].rearrange("p t (f l) -> p t f l", l=LA), axis=AX.X, op=ALU.add
                ).then_inc(small_summed, 1)
                nc.vector.tensor_reduce(
                    s[:, 0:nt, A_SLOTS:SMALL],
                    picked[:, 0:nt, 2 * A_COLS:2 * A_COLS + B_SLOTS * LB].rearrange("p t (f l) -> p t f l", l=LB),
                    axis=AX.X, op=ALU.add).then_inc(small_summed, 1)

            def pick_middle(c):
                for t in range(CHUNK_TILES[c]):
                    n = CANDIDATE_USE["middle", c, t]
                    dve.wait_ge(candidates_read, n - 1)
                    dve.wait_ge(candidates_ready, n + 1)
                    for m in range(CHUNK_SELECTED[c]):
                        slot = SMALL + m
                        last = nc.vector.scalar_tensor_tensor(
                            picked_middle[:, n % 2, m], count_middle[:], lo[:, FIRST_TILE[c] + t, slot:slot + 1],
                            cand_ps[:, n % 2, m * LM:(m + 1) * LM], op0=ALU.is_equal, op1=ALU.mult,
                            accum_out=sums[:, c % 2, t, slot:slot + 1])
                    last.then_inc(candidates_read, 1)

            def multiply_pairs(c):
                nt = CHUNK_TILES[c]
                s = sums[:, c % 2, 0:nt]
                first_gathered = SMALL + CHUNK_SELECTED[c]
                dve.wait_ge(rows_gathered[c], 16 * nt * (FIELDS - first_gathered))
                nc.vector.tensor_reduce(s[:, :, first_gathered:FIELDS], gathered(c), axis=AX.X,
                                        op=ALU.add).then_inc(rows_summed, 1)
                dve.wait_ge(small_summed, 2 * c + 2)
                nc.vector.tensor_copy(s[:, :, FIELDS:FIELDS + HALF], s[:, :, 0:HALF]).then_inc(sums_extended, 1)
                dve.wait_ge(rows_summed, c + 1)
                if CHUNK_SELECTED[c]:
                    dve.wait_ge(candidates_read, CANDIDATE_USE["middle", c, nt - 1] + 1)
                dve.wait_ge(sums_extended, c + 1)
                if c >= 2:
                    dve.wait_ge(z_transposed, K1 * (c - 1))
                row = s.ap[0]
                pitch = FIELDS + HALF
                first = bass.AP(tensor=s.tensor, offset=s.offset, ap=[list(row), [pitch, nt], [0, RING], [1, FIELDS]])
                second = bass.AP(tensor=s.tensor, offset=s.offset + 1,
                                 ap=[list(row), [pitch, nt], [1, RING], [1, FIELDS]])
                nc.vector.tensor_tensor(
                    z[:, c % 2, 0:nt, 0:RING * FIELDS].rearrange("p t (d i) -> p t d i", d=RING),
                    first, second, op=ALU.mult).then_inc(z_ready, 1)
                nc.vector.tensor_tensor(z[:, c % 2, 0:nt, RING * FIELDS:PAIRS], s[:, :, 0:HALF], s[:, :, HALF:FIELDS],
                                        op=ALU.mult).then_inc(z_ready, 1)

            def split_z(c):
                cols = CHUNK_TILES[c] * P
                for k in range(K1):
                    n = c * K1 + k
                    dve.wait_ge(zt_hi_ready, n + 1)
                    nc.vector.tensor_tensor(zt_lo[:, k, 0:cols], zt_ps[:, n % 2, 0:cols],
                                            zt_hi[:, k, 0:cols].bitcast(f32), op=ALU.subtract).then_inc(zt_lo_ready, 1)

            nc.vector.memset(small_parts[:], 0.0).then_inc(parts_cleared, 1)
            dve.wait_ge(ids_by_slot_loaded, 16)
            halves = slot_ids[:, 0:BATCH]
            nc.vector.tensor_scalar(halves, halves, 1, None, op0=ALU.logical_shift_right).then_inc(hi_steps, 1)
            dve.wait_ge(hi_steps, 1)
            dve.wait_ge(multipliers_loaded, 16)
            nc.vector.tensor_scalar(halves, halves, multiplier[:], None, op0=ALU.mult).then_inc(hi_steps, 1)
            dve.wait_ge(hi_steps, 2)
            nc.vector.tensor_scalar(halves, halves, SHIFT, None, op0=ALU.logical_shift_right).then_inc(hi_steps, 1)
            dve.wait_ge(ids_loaded, 16)
            nc.vector.tensor_scalar(hi_int[:], ids_sb[:, :, 0:SEL_SLOTS], 1, None,
                                    op0=ALU.logical_shift_right).then_inc(lo_steps, 1)
            dve.wait_ge(lo_steps, 1)
            classes = ((0, A_SLOTS, LA), (A_SLOTS, SMALL, LB), (SMALL, SEL_SLOTS, LM))
            for s0, s1, length in classes:
                nc.vector.tensor_scalar(hi_int[:, :, s0:s1], hi_int[:, :, s0:s1], float(MULTIPLIER[length]), None,
                                        op0=ALU.mult).then_inc(lo_steps, 1)
            dve.wait_ge(lo_steps, 4)
            nc.vector.tensor_scalar(hi_int[:], hi_int[:], SHIFT, None, op0=ALU.logical_shift_right).then_inc(lo_steps, 1)
            dve.wait_ge(lo_steps, 5)
            for s0, s1, length in classes:
                nc.vector.scalar_tensor_tensor(lo[:, :, s0:s1], hi_int[:, :, s0:s1], float(-length),
                                               ids_sb[:, :, s0:s1], op0=ALU.mult, op1=ALU.add).then_inc(lo_steps, 1)
            for n in range(SMALL_PIECES):
                sum_piece(n)
            dve.wait_ge(piece_summed, SMALL_PIECES)
            dve.wait_ge(parts_cleared, 1)
            step = split([(h * 64, h * 64 + 64, src, dst + h * n, n)
                          for src, dst, n in ((0, 0, A_COLS), (A_COLS, 2 * A_COLS, B_COLS)) for h in range(2)],
                         small_parts, 0)
            dve.wait_ge(lo_steps, 8)
            dve.wait_ge(constants_ready, 6)
            make_hot(0)
            pick_small(0)
            make_hot(1)
            pick_small(1)
            sum_piece(4)
            sum_piece(5)
            dve.wait_ge(w1_hi_ready, 1)
            nc.vector.tensor_tensor(w1_lo[:], h1[:], w1_hi[:].bitcast(f32), op=ALU.subtract).then_inc(w1_lo_ready, 1)
            multiply_pairs(0)
            split_z(0)
            make_hot(2)
            pick_small(2)
            for n in range(6, len(PIECES)):
                sum_piece(n)
            dve.wait_ge(piece_summed, len(PIECES))
            split([(0, P, S_COLS, 0, M_SEL * LM)], middle_parts, step)
            pick_middle(1)
            multiply_pairs(1)
            split_z(1)
            make_hot(3)
            pick_small(3)
            pick_middle(2)
            multiply_pairs(2)
            split_z(2)
            make_hot(4)
            pick_small(4)
            pick_middle(3)
            multiply_pairs(3)
            split_z(3)
            pick_middle(4)
            multiply_pairs(4)
            split_z(4)

        @block.scalar
        def _(act):
            def copy_hi(c):
                cols = CHUNK_TILES[c] * P
                if c >= 2:
                    act.wait_ge(candidates_ready, CANDIDATE_USE[_small(c - 2)[-1]] + 1)
                    if CHUNK_SELECTED[c - 2]:
                        act.wait_ge(candidates_ready, CANDIDATE_USE[_middle(c - 2)[-1]] + 1)
                for use in _hi(c):
                    n, g = BANK_USE[use], use[2]
                    to = small_hot[:, c % 2, g, 0:cols] if g < S_GROUPS else middle_hot[:, c % 2, g - S_GROUPS, 0:cols]
                    act.wait_ge(bank_filled, n + 1)
                    nc.scalar.copy(to, bank_ps[:, n % BANKS, 0:cols]).then_inc(bank_read, 1)

            def run_chunk(c):
                nt, t0 = CHUNK_TILES[c], FIRST_TILE[c]
                cols = nt * P
                if c >= 2:
                    act.wait_ge(z_transposed, K1 * (c - 1))
                nc.scalar.copy(z[:, c % 2, 0:nt, PAIRS:], dense_sb[:, t0:t0 + nt, :]).then_inc(dense_placed, 1)
                for k in range(K1):
                    n = c * K1 + k
                    act.wait_ge(z_transposed, n + 1)
                    nc.scalar.copy(zt_hi[:, k, 0:cols], zt_ps[:, n % 2, 0:cols]).then_inc(zt_hi_ready, 1)
                for m in range(K2):
                    n = BANK_USE["l1", c, m]
                    act.wait_ge(bank_filled, n + 1)
                    nc.scalar.activation(h1[:, m, 0:cols], bank_ps[:, n % BANKS, 0:cols], ACT.Relu,
                                         bias=b1[:, m:m + 1]).then_inc(bank_read, 1)
                for m in range(K3):
                    n = BANK_USE["l2", c, m]
                    act.wait_ge(bank_filled, n + 1)
                    nc.scalar.activation(h2[:, m, 0:cols], bank_ps[:, n % BANKS, 0:cols], ACT.Relu,
                                         bias=b2[:, m:m + 1]).then_inc(bank_read, 1)
                n = BANK_USE["l3", c, 0]
                act.wait_ge(bank_filled, n + 1)
                if c >= 2:
                    act.wait_ge(y_stored[c % 2], 16 * (c // 2))
                nc.scalar.copy(y_sb[0:1, c % 2, 0:cols], bank_ps[0:1, n % BANKS, 0:cols]).then_inc(bank_read, 1)

            act.dma_start(selectors_in, selectors).then_inc(selectors_loaded, 16)
            act.dma_start(multiplier[:], multipliers).then_inc(multipliers_loaded, 16)
            act.wait_ge(selectors_loaded, 16)
            nc.scalar.copy(selector[:].rearrange("p g l -> p (g l)"), selectors_in).then_inc(selector_ready, 1)
            act.wait_ge(hi_steps, 3)
            nc.scalar.copy(hi_by_slot[:], slot_ids[:, 0:BATCH]).then_inc(hi_ready, 1)
            copy_hi(0)
            act.wait_ge(w1_loaded, 16)
            nc.scalar.copy(w1_hi[:], h1[:]).then_inc(w1_hi_ready, 1)
            copy_hi(1)
            copy_hi(2)
            act.wait_ge(dense_loaded, 16)
            act.wait_ge(hi_ready, 1)
            act.wait_ge(weights_loaded, 16)
            act.wait_ge(w1_lo_ready, 1)
            run_chunk(0)
            copy_hi(3)
            run_chunk(1)
            copy_hi(4)
            run_chunk(2)
            run_chunk(3)
            run_chunk(4)

        @block.tensor
        def _(pe):
            def take_bank(n):
                if n >= BANKS:
                    pe.wait_ge(bank_read, n - BANKS + 1)
                return bank_ps[:, n % BANKS]

            def broadcast_hi(c):
                first, cols = FIRST_TILE[c] * P, CHUNK_TILES[c] * P
                for use in _hi(c):
                    bank = take_bank(BANK_USE[use])
                    nc.tensor.matmul(bank[:, 0:cols], selector[:, use[2], :], hi_by_slot[:, first:first + cols],
                                     start=True, stop=True).then_inc(bank_filled, 1)

            def select(use):
                kind, c, t = use
                n = CANDIDATE_USE[use]
                if n >= 2:
                    pe.wait_ge(candidates_read, n - 1)
                made = sum(1 + (CHUNK_SELECTED[x] > 0) for x in range(c)) + (1 if kind == "small" else 2)
                pe.wait_ge(hot_ready, made)
                pe.wait_ge(parts_ready, 1 if kind == "small" else 2)
                bank = cand_ps[:, n % 2]
                lanes = slice(t * P, (t + 1) * P)
                if kind == "small":
                    for g in range(S_GROUPS):
                        if g < A_GROUPS:
                            at, pitch, length, col = 0, A_COLS, LA, g * LA
                        else:
                            at, pitch, length, col = 2 * A_COLS, B_COLS, LB, (g - A_GROUPS) * LB
                        for r in range(3):
                            to, by = (x[:, at:at + 2 * pitch].rearrange("p (h c) -> p h c", h=2)[:, :, col:col + length]
                                      for x in (bank, small_parts[:, r]))
                            last = nc.tensor.matmul(to, small_hot[:, c % 2, g, lanes], by, start=r == 0, stop=r == 2)
                else:
                    for m in range(CHUNK_SELECTED[c]):
                        for r in range(3):
                            last = nc.tensor.matmul(bank[:, m * LM:(m + 1) * LM], middle_hot[:, c % 2, m, lanes],
                                                    middle_parts[:, r, m * LM:(m + 1) * LM], start=r == 0, stop=r == 2)
                last.then_inc(candidates_ready, 1)

            def run_chunk(c):
                nt = CHUNK_TILES[c]
                cols = nt * P
                between = list(BETWEEN[c])
                steps = K2 + K3

                def fill(step):
                    for use in between[len(between) * step // steps:len(between) * (step + 1) // steps]:
                        select(use)

                pe.wait_ge(z_ready, 2 * c + 2)
                pe.wait_ge(dense_placed, c + 1)
                for k in range(K1):
                    n = c * K1 + k
                    if n >= 2:
                        pe.wait_ge(zt_lo_ready, n - 1)
                    for t in range(nt):
                        last = nc.tensor.transpose(zt_ps[:, n % 2, t * P:(t + 1) * P],
                                                   z[:, c % 2, t, k * P:(k + 1) * P], identity)
                    last.then_inc(z_transposed, 1)
                for m in range(K2):
                    bank = take_bank(BANK_USE["l1", c, m])[:, 0:cols]
                    for k in range(K1):
                        if m == 0:
                            pe.wait_ge(zt_lo_ready, c * K1 + k + 1)
                        w_hi, w_lo = (w[:, k, m * P:(m + 1) * P] for w in (w1_hi, w1_lo))
                        z_hi, z_lo = zt_hi[:, k, 0:cols], zt_lo[:, k, 0:cols]
                        nc.tensor.matmul(bank, w_hi, z_hi, start=k == 0, stop=False)
                        nc.tensor.matmul(bank, w_hi, z_lo, start=False, stop=False)
                        last = nc.tensor.matmul(bank, w_lo, z_hi, start=False, stop=k == K1 - 1)
                    last.then_inc(bank_filled, 1)
                    fill(m)
                for m in range(K3):
                    bank = take_bank(BANK_USE["l2", c, m])[:, 0:cols]
                    for k in range(K2):
                        pe.wait_ge(bank_read, BANK_USE["l1", c, k] + 1)
                        last = nc.tensor.matmul(bank, w2[:, k, m * P:(m + 1) * P], h1[:, k, 0:cols],
                                                start=k == 0, stop=k == K2 - 1)
                    last.then_inc(bank_filled, 1)
                    fill(K2 + m)
                bank = take_bank(BANK_USE["l3", c, 0])
                for k in range(K3):
                    pe.wait_ge(bank_read, BANK_USE["l2", c, k] + 1)
                    last = nc.tensor.matmul(bank[0:1, 0:cols], w3[:, k:k + 1], h2[:, k, 0:cols],
                                            start=k == 0, stop=k == K3 - 1)
                last.then_inc(bank_filled, 1)

            pe.wait_ge(selector_ready, 1)
            pe.wait_ge(hi_ready, 1)
            broadcast_hi(0)
            broadcast_hi(1)
            for use in _small(0):
                select(use)
            broadcast_hi(2)
            for use in _small(1):
                select(use)
            pe.wait_ge(weights_loaded, 16)
            pe.wait_ge(w1_lo_ready, 1)
            run_chunk(0)
            for use in _middle(1):
                select(use)
            broadcast_hi(3)
            run_chunk(1)
            broadcast_hi(4)
            run_chunk(2)
            run_chunk(3)
            run_chunk(4)


def kernel(**inputs):
    import numpy as _np
    import concourse.bacc as _bacc
    from concourse import mybir as _mybir
    from concourse.bass_utils import run_bass_kernel_spmd as _run

    nc = _bacc.Bacc("TRN2", target_bir_lowering=False, num_devices=1)
    arrays = {}

    def put(name, a):
        arrays[name] = a = _np.ascontiguousarray(a)
        return nc.dram_tensor(name, a.shape, _mybir.dt.from_np(a.dtype), kind="ExternalInput").ap()

    tables = [_np.asarray(inputs[f"tbl_{f}"]) for f in SLOTS]

    def streamed(slots, halves, lanes, length):
        groups = len(slots) // halves
        a = _np.zeros((halves, groups, lanes * length, EMBED), _np.float32)
        for n, slot in enumerate(slots):
            if slot is not None:
                a[n // groups, n % groups, :len(tables[slot])] = tables[slot]
        a = a.reshape(halves, groups, lanes, length, EMBED).transpose(0, 2, 1, 3, 4)
        return a.reshape(halves * lanes, groups * length * EMBED)

    row_of = {}
    for i in range(FIELDS - 1):
        for j in range(i + 1, FIELDS):
            row_of[i, j] = row_of[j, i] = len(row_of) // 2
    order = [row_of[SLOTS[i], SLOTS[j]] for i, j in pair_order()] + list(range(PAIRS, PAIRS + DENSE))

    def by_partition(w):
        w = _np.asarray(w).reshape(-1, P, w.shape[-1] if w.ndim > 1 else 1)
        return w.transpose(1, 0, 2).reshape(P, -1)

    weights = _np.concatenate(
        [by_partition(inputs[n]) for n in ("W_top2", "W_top3", "b_top1", "b_top2")]
        + [_np.eye(P, dtype=_np.float32)], axis=1)

    selectors = _np.zeros((SEL_SLOTS, GROUPS * P), _np.float32)
    multipliers = _np.zeros((SEL_SLOTS, 1), _np.float32)
    for slot in range(SEL_SLOTS):
        if slot < A_SLOTS:
            h, g, length = slot // A_GROUPS, slot % A_GROUPS, LA
        elif slot < SMALL:
            h, g, length = (slot - A_SLOTS) // B_GROUPS, A_GROUPS + (slot - A_SLOTS) % B_GROUPS, LB
        else:
            h, g, length = 0, S_GROUPS + slot - SMALL, LM
        first = g * P + h * 64
        selectors[slot, first:first + (64 if slot < SMALL else P)] = 1
        multipliers[slot, 0] = MULTIPLIER[length]

    ids = _np.asarray(inputs["ids"])[:, SLOTS]
    by_slot = ids[:, :SEL_SLOTS].T.reshape(SEL_SLOTS, P, TILES).transpose(0, 2, 1).reshape(SEL_SLOTS, BATCH)
    gathered_tables = [put(f"table_{s}", tables[s]) if s >= SMALL + min(CHUNK_SELECTED) else None
                       for s in range(FIELDS)]
    build_program(
        nc, put("ids", ids), put("ids_by_slot", by_slot), put("dense_ctx", inputs["dense_ctx"]),
        put("w1", by_partition(_np.asarray(inputs["W_top1"])[order])), put("weights", weights),
        put("selectors", selectors), put("multipliers", multipliers),
        put("rows_a", streamed(list(range(A_SLOTS)), 2, 64, LA)),
        put("rows_b", streamed(list(range(A_SLOTS, SMALL)) + [None], 2, 64, LB)),
        [put(f"rows_m{m}", streamed([SMALL + m], 1, P, LM)) for m in range(M_SEL)],
        gathered_tables,
        nc.dram_tensor("out", (1, BATCH), _mybir.dt.float32, kind="ExternalOutput").ap())
    r = _run(nc, [arrays], core_ids=[0])
    return r.results[0]["out"].reshape(TILES, P).T.reshape(BATCH, 1)
```

```python
from contextlib import ExitStack

import concourse.bass as bass
from concourse import mybir

P = 128
BATCH = 2048
FIELDS = 32
EMBED = 64
DENSE = 16
PAIRS = FIELDS * (FIELDS - 1) // 2
H1 = 512
H2 = 256
TILES = BATCH // P
K1 = (PAIRS + DENSE) // P
K2 = H1 // P
K3 = H2 // P
HALF = FIELDS // 2
RING = HALF - 1

VOCAB = [1000, 125000, 1250, 1250, 1250, 125000, 1000, 12500, 1250, 12500, 1000, 12500, 1000, 12500, 1000, 125000,
         12500, 1000, 12500, 1250, 1250, 1250, 1000, 1000, 1000, 12500, 12500, 1000, 1250, 1000, 1250, 1000]
SLOTS = [f for v in (1000, 1250, 12500, 125000) for f in range(FIELDS) if VOCAB[f] == v]

CHUNK_TILES = [2, 2, 2, 3, 3, 2, 2]
CHUNK_SELECTED = [0, 0, 2, 3, 4, 4, 4]
CHUNKS = len(CHUNK_TILES)
FIRST_TILE = [sum(CHUNK_TILES[:c]) for c in range(CHUNKS)]
CT = max(CHUNK_TILES)
CHUNK = CT * P

A_SLOTS = VOCAB.count(1000)
B_SLOTS = VOCAB.count(1250)
SMALL = A_SLOTS + B_SLOTS
M_SEL = max(CHUNK_SELECTED)
A_GROUPS = A_SLOTS // 2
B_GROUPS = (B_SLOTS + 1) // 2
S_GROUPS = A_GROUPS + B_GROUPS
SEL_SLOTS = SMALL + M_SEL
LA, LB, LM = 16, 20, 98
A_COLS = A_GROUPS * LA
B_COLS = B_GROUPS * LB
S_COLS = A_COLS + B_COLS
V_SMALL = 2 * S_COLS
RS_COLS = S_COLS + M_SEL * LM

SHIFT = 17
MULTIPLIER = {LA: 16384, LB: 13108, LM: 2675}
for _length, _rows in ((LA, 1000), (LB, 1250), (LM, 12500)):
    assert (_rows >> 1) * MULTIPLIER[_length] < 1 << 24
    assert all(((r >> 1) * MULTIPLIER[_length]) >> SHIFT == r // _length for r in range(_rows))

HALF_ROW = EMBED // 2
BLOCKS = [("a", j * A_COLS // 2, A_COLS // 2) for j in range(2)]
BLOCKS += [("b", A_COLS + at, n) for at, n in ((0, 2 * B_COLS // 5), (2 * B_COLS // 5, 2 * B_COLS // 5),
                                               (4 * B_COLS // 5, B_COLS - 4 * B_COLS // 5))]
A_BLOCKS = 2
SMALL_BLOCKS = len(BLOCKS)
BLOCKS += [("m", S_COLS + m * LM, LM) for m in range(M_SEL)]
BLOCK_SLOTS = 4
BLOCK_VALUES = max(n * (HALF_ROW if kind == "m" else EMBED) for kind, _, n in BLOCKS)
ADD_AFTER = [39, 44, 59, 66]
MIDDLE_SUMS = {(2, "before small picks"): 0, (2, "after small picks"): 1, (3, "between small picks"): 2,
               (4, "between small picks"): 3}
MIDDLE_SUM_PARTS = 2
assert [*MIDDLE_SUMS.values()] == list(range(M_SEL)) and len(ADD_AFTER) == M_SEL
assert all(CHUNK_SELECTED[c] <= sum(at[0] <= c for at in MIDDLE_SUMS) for c in range(CHUNKS))
HOT_EARLY_FROM = 3
LOAD_AFTER_GATHERS = 1
CCE_VALUES = 2048

BY_HALF = (list(range(A_GROUPS)) + list(range(A_SLOTS, A_SLOTS + B_GROUPS))
           + list(range(A_GROUPS, A_SLOTS)) + list(range(A_SLOTS + B_GROUPS, SMALL)) + [None]
           + list(range(SMALL, SEL_SLOTS)))

W2_AT = 0
W3_AT = W2_AT + K2 * H2
B1_AT = W3_AT + K3
B2_AT = B1_AT + K2
ID_AT = B2_AT + K3
WEIGHT_COLS = ID_AT + P

GATHER_BUFFERS = 3
GATHERED = [CHUNK_TILES[c] * (FIELDS - SMALL - CHUNK_SELECTED[c]) for c in range(CHUNKS)]
GATHER_ROWS = [max(GATHERED[s::GATHER_BUFFERS]) for s in range(GATHER_BUFFERS)]

SPLIT_LAYER2 = (5, 6)

BANK = 512
BANKS = 3
BANK_ORDER = [(layer, c, m) for c in range(CHUNKS) for layer, n in (("l1", K2), ("l2", K3)) for m in range(n)]
BANK_USE = {use: n for n, use in enumerate(BANK_ORDER)}


def _small(c):
    return [("small", c, t) for t in range(CHUNK_TILES[c])]


def _middle(c):
    return [("middle", c, t) for t in range(CHUNK_TILES[c] if CHUNK_SELECTED[c] else 0)]


CANDIDATE_ORDER = [use for c in range(CHUNKS) for use in _small(c) + _middle(c)]
CANDIDATE_USE = {use: n for n, use in enumerate(CANDIDATE_ORDER)}

SMALL_SPLIT_STEPS = 2 * 2 * (3 + 2)
MIDDLE_SPLIT_STEPS = 3 + 2


def h1_parts_before(c):
    return K2 * sum(x < c for x in SPLIT_LAYER2)


def pair_order():
    return [(i, (i + d) % FIELDS) for d in range(1, HALF) for i in range(FIELDS)] + [
        (i, i + HALF) for i in range(HALF)]


def build_program(nc, ids, ids_by_slot, dense, w1, weights, multipliers, rows_a, rows_b, rows_m, tables, hi_dram, out):
    f32 = mybir.dt.float32
    f32r = mybir.dt.float32r
    bf16 = mybir.dt.bfloat16
    i32 = mybir.dt.int32
    ALU = mybir.AluOpType
    ACT = mybir.ActivationFunctionType
    AX = mybir.AxisListType

    with ExitStack() as stack:
        hold = stack.enter_context
        ids_sb = hold(nc.sbuf_tensor([P, TILES, FIELDS], i32))
        hi_int = hold(nc.sbuf_tensor([P, TILES, SEL_SLOTS], i32))
        lo = hold(nc.sbuf_tensor([P, TILES, SEL_SLOTS], f32))
        lo_small = hold(nc.sbuf_tensor([P, TILES, A_SLOTS + 2 * B_GROUPS], bf16))
        hi_by_slot = hold(nc.sbuf_tensor([len(BY_HALF), BATCH], bf16))
        multiplier = hold(nc.sbuf_tensor([len(BY_HALF), 1], f32))
        blocks = hold(nc.sbuf_tensor([P, BLOCK_SLOTS, BLOCK_VALUES], f32))
        row_sums = hold(nc.sbuf_tensor([P, RS_COLS], f32))
        rest = hold(nc.sbuf_tensor([P, RS_COLS], f32))
        small_parts = hold(nc.sbuf_tensor([P, 3, V_SMALL], bf16))
        middle_parts = hold(nc.sbuf_tensor([P, 3, M_SEL * LM], bf16))
        small_hot = hold(nc.sbuf_tensor([P, 2, S_GROUPS, CHUNK], bf16))
        middle_hot = hold(nc.sbuf_tensor([P, 2, M_SEL, CHUNK], bf16))
        lo_hot = hold(nc.sbuf_tensor([P, CT, V_SMALL], bf16))
        picked = hold(nc.sbuf_tensor([P, CT, V_SMALL], f32))
        picked_middle = hold(nc.sbuf_tensor([P, 2, M_SEL, LM], bf16))
        lane64 = hold(nc.sbuf_tensor([P, 1], f32))
        lane128 = hold(nc.sbuf_tensor([P, 1], f32))
        count_small = hold(nc.sbuf_tensor([P, V_SMALL], bf16))
        count_middle = hold(nc.sbuf_tensor([P, LM], f32))
        gathered = hold(nc.sbuf_tensor([P, sum(GATHER_ROWS), EMBED], f32))
        sums = hold(nc.sbuf_tensor([P, 2, CT, FIELDS + HALF], f32))
        dense_sb = hold(nc.sbuf_tensor([P, TILES, DENSE], f32))
        w_sb = hold(nc.sbuf_tensor([P, WEIGHT_COLS], f32))
        w1_hi = hold(nc.sbuf_tensor([P, K1, H1], f32r))
        w1_lo = hold(nc.sbuf_tensor([P, K1, H1], f32r))
        z = hold(nc.sbuf_tensor([P, 2, CT, PAIRS + DENSE], f32))
        zt_hi = hold(nc.sbuf_tensor([P, K1, CHUNK], f32r))
        zt_lo = hold(nc.sbuf_tensor([P, K1, CHUNK], f32r))
        hidden = hold(nc.sbuf_tensor([P, K2 + K3, CHUNK], f32))
        h1_hi = hold(nc.sbuf_tensor([P, K2, CHUNK], f32r))
        h1_lo = hold(nc.sbuf_tensor([P, K2, CHUNK], f32r))
        w2_hi = hold(nc.sbuf_tensor([P, K2, H2], f32r))
        w2_lo = hold(nc.sbuf_tensor([P, K2, H2], f32r))
        y_sb = hold(nc.sbuf_tensor([1, BATCH], f32))
        zt_ps = hold(nc.psum_tensor([P, 2, BANK], f32))
        bank_ps = hold(nc.psum_tensor([P, BANKS, BANK], f32))
        cand_ps = hold(nc.psum_tensor([P, 2, BANK], f32))
        y_ps = hold(nc.psum_tensor([1, BANK], f32))

        ids_loaded = hold(nc.semaphore("ids_loaded"))
        ids_by_slot_loaded = hold(nc.semaphore("ids_by_slot_loaded"))
        multipliers_loaded = hold(nc.semaphore("multipliers_loaded"))
        hi_stored = hold(nc.semaphore("hi_stored"))
        dense_loaded = hold(nc.semaphore("dense_loaded"))
        w1_loaded = hold(nc.semaphore("w1_loaded"))
        weights_loaded = hold(nc.semaphore("weights_loaded"))
        block_loaded = [hold(nc.semaphore(f"block_loaded_{s}")) for s in range(BLOCK_SLOTS)]
        block_added = [hold(nc.semaphore(f"block_added_{s}")) for s in range(BLOCK_SLOTS)]
        block_summed = hold(nc.semaphore("block_summed"))
        hi_spread = [hold(nc.semaphore(f"hi_spread_{s}")) for s in range(2)]
        constants_ready = hold(nc.semaphore("constants_ready"))
        parts_cleared = hold(nc.semaphore("parts_cleared"))
        hi_steps = hold(nc.semaphore("hi_steps"))
        lo_steps = hold(nc.semaphore("lo_steps"))
        hi_ready = hold(nc.semaphore("hi_ready"))
        split_steps = hold(nc.semaphore("split_steps"))
        hot_ready = hold(nc.semaphore("hot_ready"))
        lo_hot_ready = hold(nc.semaphore("lo_hot_ready"))
        candidates_ready = hold(nc.semaphore("candidates_ready"))
        candidates_read = hold(nc.semaphore("candidates_read"))
        rows_gathered = [hold(nc.semaphore(f"rows_gathered_{c}")) for c in range(CHUNKS)]
        small_summed = hold(nc.semaphore("small_summed"))
        rows_summed = hold(nc.semaphore("rows_summed"))
        sums_extended = hold(nc.semaphore("sums_extended"))
        w1_hi_ready = hold(nc.semaphore("w1_hi_ready"))
        w2_hi_ready = hold(nc.semaphore("w2_hi_ready"))
        w2_lo_ready = hold(nc.semaphore("w2_lo_ready"))
        h1_hi_ready = hold(nc.semaphore("h1_hi_ready"))
        h1_lo_ready = hold(nc.semaphore("h1_lo_ready"))
        w1_lo_ready = hold(nc.semaphore("w1_lo_ready"))
        z_ready = hold(nc.semaphore("z_ready"))
        dense_placed = hold(nc.semaphore("dense_placed"))
        z_transposed = hold(nc.semaphore("z_transposed"))
        zt_hi_ready = hold(nc.semaphore("zt_hi_ready"))
        zt_lo_ready = hold(nc.semaphore("zt_lo_ready"))
        bank_filled = hold(nc.semaphore("bank_filled"))
        bank_read = hold(nc.semaphore("bank_read"))
        y_filled = hold(nc.semaphore("y_filled"))
        y_read = hold(nc.semaphore("y_read"))
        y_stored = hold(nc.semaphore("y_stored"))
        block = hold(nc.Block())

        w2 = w_sb[:, W2_AT:W3_AT].rearrange("p (k m) -> p k m", k=K2)
        w3 = w_sb[:, W3_AT:B1_AT]
        b1 = w_sb[:, B1_AT:B2_AT]
        b2 = w_sb[:, B2_AT:ID_AT]
        identity = w_sb[:, ID_AT:ID_AT + P]
        slot_ids = z[0:len(BY_HALF)].rearrange("p b t k -> p (b t k)").bitcast(i32)
        w1_whole = hidden[:].rearrange("p k n -> p (k n)")[:, 0:K1 * H1]
        h1, h2 = hidden[:, 0:K2], hidden[:, K2:K2 + K3]

        def gathered_rows(c):
            first = sum(GATHER_ROWS[:c % GATHER_BUFFERS])
            return gathered[:, first:first + GATHERED[c], :].rearrange("p (t s) e -> p t s e", t=CHUNK_TILES[c])

        def additions(n):
            return sum(BLOCKS[x][0] == "m" for x in range(n % BLOCK_SLOTS, n + 1, BLOCK_SLOTS))

        def sums_through(n):
            return n + 1 if n < SMALL_BLOCKS else SMALL_BLOCKS + (n + 1 - SMALL_BLOCKS) * MIDDLE_SUM_PARTS

        @block.sync
        def _(sp):
            def load_block(n):
                kind, first, cols = BLOCKS[n]
                if n >= BLOCK_SLOTS:
                    sp.wait_ge(block_summed, sums_through(n - BLOCK_SLOTS))
                if kind == "m":
                    source = rows_m[n - SMALL_BLOCKS][0]
                else:
                    rows, at = (rows_a, first) if kind == "a" else (rows_b, first - A_COLS)
                    source = rows[:, at * EMBED:(at + cols) * EMBED]
                sp.dma_start(blocks[:, n % BLOCK_SLOTS, 0:source.shape[1]],
                             source).then_inc(block_loaded[n % BLOCK_SLOTS], 16)

            sp.dma_start(slot_ids[:, 0:BATCH], ids_by_slot).then_inc(ids_by_slot_loaded, 16)
            sp.wait_ge(ids_loaded, 16)
            for n in range(SMALL_BLOCKS):
                load_block(n)
            sp.dma_start(w1_whole, w1).then_inc(w1_loaded, 16)
            sp.wait_ge(hi_spread[0], 32)
            sp.dma_start(w_sb[:], weights).then_inc(weights_loaded, 16)
            sp.dma_start(dense_sb[:], dense).then_inc(dense_loaded, 16)
            for n in range(SMALL_BLOCKS, len(BLOCKS)):
                if n == SMALL_BLOCKS + LOAD_AFTER_GATHERS:
                    sp.wait_ge(rows_gathered[0], 16 * GATHERED[0])
                if n >= SMALL_BLOCKS + 2:
                    sp.wait_ge(block_added[(n - 2) % BLOCK_SLOTS], 16 * additions(n - 2))
                load_block(n)
            sp.wait_ge(y_read, CHUNKS)
            sp.dma_start(out.rearrange("b o -> o b"), y_sb[:]).then_inc(y_stored, 16)
            sp.wait_ge(y_stored, 16)

        @block.gpsimd
        def _(pool):
            def add_second_halves(n):
                values = BLOCKS[n][2] * HALF_ROW
                pool.wait_ge(block_loaded[n % BLOCK_SLOTS], 16 * (n // BLOCK_SLOTS + 1))
                pool.dma_start(blocks[:, n % BLOCK_SLOTS, 0:values], rows_m[n - SMALL_BLOCKS][1], accum_op=ALU.add,
                               max_dma_last_dim=4 * CCE_VALUES).then_inc(block_added[n % BLOCK_SLOTS], 16)

            for h in range(2):
                nc.gpsimd.iota(lane64[h * 64:h * 64 + 64, :], [[0, 1]], 0, 1,
                               allow_small_or_imprecise_dtypes=True).then_inc(constants_ready, 1)
            pool.wait_ge(constants_ready, 2)
            nc.gpsimd.iota(lane128[:], [[0, 1]], 0, 1, allow_small_or_imprecise_dtypes=True).then_inc(constants_ready, 1)
            nc.gpsimd.iota(count_small[:, 0:2 * A_COLS], [[1, LA], [0, 2 * A_GROUPS]], 0, 0,
                           allow_small_or_imprecise_dtypes=True).then_inc(constants_ready, 1)
            nc.gpsimd.iota(count_small[:, 2 * A_COLS:], [[1, LB], [0, 2 * B_GROUPS]], 0, 0,
                           allow_small_or_imprecise_dtypes=True).then_inc(constants_ready, 1)
            nc.gpsimd.iota(count_middle[:], [[1, LM]], 0, 0,
                           allow_small_or_imprecise_dtypes=True).then_inc(constants_ready, 1)
            pool.wait_ge(ids_loaded, 16)
            started = 0
            for c in range(CHUNKS):
                rows = gathered_rows(c)
                if c >= GATHER_BUFFERS:
                    pool.wait_ge(rows_summed, c - GATHER_BUFFERS + 1)
                for t in range(CHUNK_TILES[c]):
                    for n, slot in enumerate(range(SMALL + CHUNK_SELECTED[c], FIELDS)):
                        if started in ADD_AFTER:
                            add_second_halves(SMALL_BLOCKS + ADD_AFTER.index(started))
                        started += 1
                        pool.indirect_dma_start(
                            rows[:, t, n, :], None, tables[slot],
                            bass.IndirectOffsetOnAxis(ap=ids_sb[:, FIRST_TILE[c] + t, slot:slot + 1], axis=0),
                        ).then_inc(rows_gathered[c], 16)

        @block.vector
        def _(dve):
            def sum_block(n, parts=None):
                kind, at, cols = BLOCKS[n]
                if kind == "m":
                    row, total = HALF_ROW, MIDDLE_SUM_PARTS
                    dve.wait_ge(block_added[n % BLOCK_SLOTS], 16 * additions(n))
                else:
                    row, total = EMBED, 1
                    dve.wait_ge(block_loaded[n % BLOCK_SLOTS], 16 * (n // BLOCK_SLOTS + 1))
                for part in parts or range(total):
                    first, end = cols * part // total, cols * (part + 1) // total
                    nc.vector.tensor_reduce(
                        row_sums[:, at + first:at + end],
                        blocks[:, n % BLOCK_SLOTS, first * row:end * row].rearrange("p (c e) -> p c e", e=row),
                        axis=AX.X, op=ALU.add).then_inc(block_summed, 1)

            def split(regions, parts, step):
                for r in range(3):
                    source = row_sums if r == 0 else rest
                    for p0, p1, src, dst, n in regions:
                        nc.vector.tensor_copy(parts[p0:p1, r, dst:dst + n],
                                              source[p0:p1, src:src + n]).then_inc(split_steps, 1)
                    step += len(regions)
                    dve.wait_ge(split_steps, step)
                    if r < 2:
                        for p0, p1, src, dst, n in regions:
                            nc.vector.tensor_tensor(rest[p0:p1, src:src + n], source[p0:p1, src:src + n],
                                                    parts[p0:p1, r, dst:dst + n],
                                                    op=ALU.subtract).then_inc(split_steps, 1)
                        step += len(regions)
                        dve.wait_ge(split_steps, step)
                return step

            def make_lo_hot(c):
                nt, t0 = CHUNK_TILES[c], FIRST_TILE[c]
                for at, first, slots, length in ((0, 0, A_SLOTS, LA), (2 * A_COLS, A_SLOTS, 2 * B_GROUPS, LB)):
                    end = at + slots * length
                    nc.vector.tensor_tensor(
                        lo_hot[:, 0:nt, at:end].rearrange("p t (l f) -> p t l f", l=length),
                        count_small[:, None, at:end].to_broadcast([P, nt, end - at]).rearrange(
                            "p t (l f) -> p t l f", l=length),
                        lo_small[:, t0:t0 + nt, None, first:first + slots].to_broadcast([P, nt, length, slots]),
                        op=ALU.is_equal).then_inc(lo_hot_ready, 1)

            def make_small_hot(c):
                dve.wait_ge(hi_spread[c % 2], 16 * sum(2 + (CHUNK_SELECTED[x] > 0) for x in range(c % 2, c + 1, 2)))
                hot = small_hot[:, c % 2, :, 0:CHUNK_TILES[c] * P]
                nc.vector.tensor_scalar(hot, hot, lane64[:], None, op0=ALU.is_equal).then_inc(hot_ready, 1)

            def make_middle_hot(c):
                if CHUNK_SELECTED[c]:
                    hot = middle_hot[:, c % 2, 0:CHUNK_SELECTED[c], 0:CHUNK_TILES[c] * P]
                    nc.vector.tensor_scalar(hot, hot, lane128[:], None, op0=ALU.is_equal).then_inc(hot_ready, 1)

            def sum_rows(c):
                nt = CHUNK_TILES[c]
                first_gathered = SMALL + CHUNK_SELECTED[c]
                dve.wait_ge(rows_gathered[c], 16 * nt * (FIELDS - first_gathered))
                nc.vector.tensor_reduce(sums[:, c % 2, 0:nt, first_gathered:FIELDS], gathered_rows(c), axis=AX.X,
                                        op=ALU.add).then_inc(rows_summed, 1)

            def sum_middle_table(chunk, place, step, parts=None):
                m = MIDDLE_SUMS.get((chunk, place))
                if m is None:
                    return step
                sum_block(SMALL_BLOCKS + m, parts)
                dve.wait_ge(block_summed, sums_through(SMALL_BLOCKS + m))
                return split([(0, P, S_COLS + m * LM, m * LM, LM)], middle_parts, step)

            def early_hot(c):
                return HOT_EARLY_FROM <= c < CHUNKS - 1 and (c, "between small picks") not in MIDDLE_SUMS

            def pick_small(c, step):
                nt = CHUNK_TILES[c]
                s = sums[:, c % 2]
                dve.wait_ge(lo_hot_ready, 2 * c + 2)
                for t in range(nt):
                    if t == 1 and (c, "between small picks") in MIDDLE_SUMS:
                        sum_block(SMALL_BLOCKS + MIDDLE_SUMS[c, "between small picks"], [0])
                    if t == nt - 1:
                        step = sum_middle_table(c, "between small picks", step, [1])
                    if t == nt - 1 and early_hot(c):
                        make_small_hot(c + 1)
                    n = CANDIDATE_USE["small", c, t]
                    dve.wait_ge(candidates_ready, n + 1)
                    nc.vector.tensor_tensor(picked[:, t], lo_hot[:, t], cand_ps[:, n % 2, 0:V_SMALL],
                                            op=ALU.mult).then_inc(candidates_read, 1)
                dve.wait_ge(candidates_read, CANDIDATE_USE["small", c, nt - 1] + 1)
                nc.vector.tensor_reduce(
                    s[:, 0:nt, 0:A_SLOTS],
                    picked[:, 0:nt, 0:2 * A_COLS].rearrange("p t (l f) -> p t f l", l=LA), axis=AX.X, op=ALU.add
                ).then_inc(small_summed, 1)
                nc.vector.tensor_reduce(
                    s[:, 0:nt, A_SLOTS:SMALL],
                    picked[:, 0:nt, 2 * A_COLS:].rearrange("p t (l f) -> p t f l", l=LB)[:, :, 0:B_SLOTS, :],
                    axis=AX.X, op=ALU.add).then_inc(small_summed, 1)
                return step

            def pick_middle(c, t0, t1):
                for t in range(t0, t1 if CHUNK_SELECTED[c] else 0):
                    n = CANDIDATE_USE["middle", c, t]
                    dve.wait_ge(candidates_read, n - 1)
                    dve.wait_ge(candidates_ready, n + 1)
                    for m in range(CHUNK_SELECTED[c]):
                        slot = SMALL + m
                        last = nc.vector.scalar_tensor_tensor(
                            picked_middle[:, n % 2, m], count_middle[:], lo[:, FIRST_TILE[c] + t, slot:slot + 1],
                            cand_ps[:, n % 2, m * LM:(m + 1) * LM], op0=ALU.is_equal, op1=ALU.mult,
                            accum_out=sums[:, c % 2, t, slot:slot + 1])
                    last.then_inc(candidates_read, 1)

            def multiply_pairs(c):
                nt = CHUNK_TILES[c]
                s = sums[:, c % 2, 0:nt]
                dve.wait_ge(small_summed, 2 * c + 2)
                nc.vector.tensor_copy(s[:, :, FIELDS:FIELDS + HALF], s[:, :, 0:HALF]).then_inc(sums_extended, 1)
                dve.wait_ge(rows_summed, c + 1)
                if CHUNK_SELECTED[c]:
                    dve.wait_ge(candidates_read, CANDIDATE_USE["middle", c, nt - 1] + 1)
                dve.wait_ge(sums_extended, c + 1)
                if c >= 2:
                    dve.wait_ge(z_transposed, K1 * (c - 1))
                row = s.ap[0]
                pitch = FIELDS + HALF
                first = bass.AP(tensor=s.tensor, offset=s.offset, ap=[list(row), [pitch, nt], [0, RING], [1, FIELDS]])
                second = bass.AP(tensor=s.tensor, offset=s.offset + 1,
                                 ap=[list(row), [pitch, nt], [1, RING], [1, FIELDS]])
                nc.vector.tensor_tensor(
                    z[:, c % 2, 0:nt, 0:RING * FIELDS].rearrange("p t (d i) -> p t d i", d=RING),
                    first, second, op=ALU.mult).then_inc(z_ready, 1)
                nc.vector.tensor_tensor(z[:, c % 2, 0:nt, RING * FIELDS:PAIRS], s[:, :, 0:HALF], s[:, :, HALF:FIELDS],
                                        op=ALU.mult).then_inc(z_ready, 1)

            def split_h1(c, m0, m1):
                cols = CHUNK_TILES[c] * P
                for m in range(m0, m1 if c in SPLIT_LAYER2 else m0):
                    dve.wait_ge(h1_hi_ready, h1_parts_before(c) + m + 1)
                    if c:
                        dve.wait_ge(bank_filled, BANK_USE["l2", c - 1, K3 - 1] + 1)
                    nc.vector.tensor_tensor(h1_lo[:, m, 0:cols], h1[:, m, 0:cols], h1_hi[:, m, 0:cols].bitcast(f32),
                                            op=ALU.subtract).then_inc(h1_lo_ready, 1)

            def split_z(c):
                cols = CHUNK_TILES[c] * P
                for k in range(K1):
                    n = c * K1 + k
                    dve.wait_ge(zt_hi_ready, n + 1)
                    nc.vector.tensor_tensor(zt_lo[:, k, 0:cols], zt_ps[:, n % 2, 0:cols],
                                            zt_hi[:, k, 0:cols].bitcast(f32), op=ALU.subtract).then_inc(zt_lo_ready, 1)

            nc.vector.memset(small_parts[:], 0.0).then_inc(parts_cleared, 1)
            dve.wait_ge(ids_by_slot_loaded, 16)
            halves = slot_ids[:, 0:BATCH]
            nc.vector.tensor_scalar(halves, halves, 1, None, op0=ALU.logical_shift_right).then_inc(hi_steps, 1)
            dve.wait_ge(hi_steps, 1)
            dve.wait_ge(multipliers_loaded, 16)
            nc.vector.tensor_scalar(halves, halves, multiplier[:], None, op0=ALU.mult).then_inc(hi_steps, 1)
            dve.wait_ge(hi_steps, 2)
            nc.vector.tensor_scalar(halves, halves, SHIFT, None, op0=ALU.logical_shift_right).then_inc(hi_steps, 1)
            dve.wait_ge(hi_steps, 3)
            nc.vector.tensor_copy(hi_by_slot[:], halves).then_inc(hi_ready, 1)
            dve.wait_ge(ids_loaded, 16)
            nc.vector.tensor_scalar(hi_int[:], ids_sb[:, :, 0:SEL_SLOTS], 1, None,
                                    op0=ALU.logical_shift_right).then_inc(lo_steps, 1)
            dve.wait_ge(lo_steps, 1)
            classes = ((0, A_SLOTS, LA), (A_SLOTS, SMALL, LB), (SMALL, SEL_SLOTS, LM))
            for s0, s1, length in classes:
                nc.vector.tensor_scalar(hi_int[:, :, s0:s1], hi_int[:, :, s0:s1], float(MULTIPLIER[length]), None,
                                        op0=ALU.mult).then_inc(lo_steps, 1)
            dve.wait_ge(lo_steps, 4)
            nc.vector.tensor_scalar(hi_int[:], hi_int[:], SHIFT, None, op0=ALU.logical_shift_right).then_inc(lo_steps, 1)
            dve.wait_ge(lo_steps, 5)
            for s0, s1, length in classes:
                nc.vector.scalar_tensor_tensor(lo[:, :, s0:s1], hi_int[:, :, s0:s1], float(-length),
                                               ids_sb[:, :, s0:s1], op0=ALU.mult, op1=ALU.add).then_inc(lo_steps, 1)
            dve.wait_ge(lo_steps, 8)
            nc.vector.tensor_copy(lo_small[:], lo[:, :, 0:A_SLOTS + 2 * B_GROUPS]).then_inc(lo_steps, 1)
            dve.wait_ge(lo_steps, 9)
            dve.wait_ge(constants_ready, 6)
            make_lo_hot(0)
            dve.wait_ge(parts_cleared, 1)
            step = 0
            for first, end, src, dst, n in ((0, A_BLOCKS, 0, 0, A_COLS),
                                            (A_BLOCKS, SMALL_BLOCKS, A_COLS, 2 * A_COLS, B_COLS)):
                for m in range(first, end):
                    sum_block(m)
                dve.wait_ge(block_summed, end)
                step = split([(h * 64, h * 64 + 64, src, dst + h * n, n) for h in range(2)], small_parts, step)
            make_small_hot(0)
            make_middle_hot(0)
            for c in range(CHUNKS):
                step = sum_middle_table(c, "before small picks", step)
                step = pick_small(c, step)
                step = sum_middle_table(c, "after small picks", step)
                if c + 1 < CHUNKS:
                    make_lo_hot(c + 1)
                pick_middle(c, 0, 1)
                if c + 1 < CHUNKS:
                    if not early_hot(c):
                        make_small_hot(c + 1)
                    make_middle_hot(c + 1)
                if c:
                    split_h1(c - 1, 0, 2)
                pick_middle(c, 1, CHUNK_TILES[c])
                if c:
                    split_h1(c - 1, 2, K2)
                step = sum_middle_table(c, "before pairs", step)
                sum_rows(c)
                multiply_pairs(c)
                if c == 0:
                    dve.wait_ge(w1_hi_ready, 1)
                    nc.vector.tensor_tensor(w1_lo[:].rearrange("p k m -> p (k m)"), w1_whole,
                                            w1_hi[:].rearrange("p k m -> p (k m)").bitcast(f32),
                                            op=ALU.subtract).then_inc(w1_lo_ready, 1)
                split_z(c)
                if c == SPLIT_LAYER2[0] - 2:
                    dve.wait_ge(w2_hi_ready, 1)
                    nc.vector.tensor_tensor(w2_lo[:], w2, w2_hi[:].bitcast(f32),
                                            op=ALU.subtract).then_inc(w2_lo_ready, 1)
            split_h1(CHUNKS - 1, 0, K2)

        @block.scalar
        def _(act):
            def spread_hi(c):
                first, n = FIRST_TILE[c] * P, CHUNK_TILES[c] * P
                if c >= 2:
                    act.wait_ge(candidates_ready, CANDIDATE_USE[_small(c - 2)[-1]] + 1)
                    if CHUNK_SELECTED[c - 2]:
                        act.wait_ge(candidates_ready, CANDIDATE_USE[_middle(c - 2)[-1]] + 1)
                for h in range(2):
                    source = hi_dram[None, h * S_GROUPS:(h + 1) * S_GROUPS, first:first + n]
                    act.dma_start(small_hot[h * 64:h * 64 + 64, c % 2, :, 0:n],
                                  source.to_broadcast([64, S_GROUPS, n])).then_inc(hi_spread[c % 2], 16)
                if CHUNK_SELECTED[c]:
                    source = hi_dram[None, 2 * S_GROUPS:2 * S_GROUPS + CHUNK_SELECTED[c], first:first + n]
                    act.dma_start(middle_hot[:, c % 2, 0:CHUNK_SELECTED[c], 0:n],
                                  source.to_broadcast([P, CHUNK_SELECTED[c], n])).then_inc(hi_spread[c % 2], 16)

            def place_dense(c):
                nt, t0 = CHUNK_TILES[c], FIRST_TILE[c]
                if c >= 2:
                    act.wait_ge(z_transposed, K1 * (c - 1))
                nc.scalar.copy(z[:, c % 2, 0:nt, PAIRS:], dense_sb[:, t0:t0 + nt, :]).then_inc(dense_placed, 1)

            def read_outputs(c):
                first, n = FIRST_TILE[c] * P, CHUNK_TILES[c] * P
                act.wait_ge(y_filled, c + 1)
                nc.scalar.copy(y_sb[:, first:first + n], y_ps[:, 0:n]).then_inc(y_read, 1)

            def run_chunk(c):
                cols = CHUNK_TILES[c] * P
                for k in range(K1):
                    n = c * K1 + k
                    act.wait_ge(z_transposed, n + 1)
                    nc.scalar.copy(zt_hi[:, k, 0:cols], zt_ps[:, n % 2, 0:cols]).then_inc(zt_hi_ready, 1)
                if c + 1 < CHUNKS:
                    place_dense(c + 1)
                if c:
                    read_outputs(c - 1)
                if c == 0:
                    spread_hi(2)
                    nc.scalar.copy(w2_hi[:], w2).then_inc(w2_hi_ready, 1)
                for m in range(K2):
                    n = BANK_USE["l1", c, m]
                    act.wait_ge(bank_filled, n + 1)
                    nc.scalar.activation(h1[:, m, 0:cols], bank_ps[:, n % BANKS, 0:cols], ACT.Relu,
                                         bias=b1[:, m:m + 1]).then_inc(bank_read, 1)
                    if c in SPLIT_LAYER2:
                        act.wait_ge(bank_read, n + 1)
                        nc.scalar.copy(h1_hi[:, m, 0:cols], h1[:, m, 0:cols]).then_inc(h1_hi_ready, 1)
                if c + 3 < CHUNKS:
                    spread_hi(c + 3)
                for m in range(K3):
                    n = BANK_USE["l2", c, m]
                    act.wait_ge(bank_filled, n + 1)
                    nc.scalar.activation(h2[:, m, 0:cols], bank_ps[:, n % BANKS, 0:cols], ACT.Relu,
                                         bias=b2[:, m:m + 1]).then_inc(bank_read, 1)

            act.dma_start(multiplier[:], multipliers).then_inc(multipliers_loaded, 16)
            act.dma_start(ids_sb[:], ids).then_inc(ids_loaded, 16)
            act.wait_ge(hi_ready, 1)
            act.dma_start(hi_dram, hi_by_slot[:]).then_inc(hi_stored, 16)
            act.wait_ge(hi_stored, 16)
            spread_hi(0)
            act.wait_ge(w1_loaded, 16)
            spread_hi(1)
            nc.scalar.copy(w1_hi[:].rearrange("p k m -> p (k m)"), w1_whole).then_inc(w1_hi_ready, 1)
            act.wait_ge(dense_loaded, 16)
            act.wait_ge(hi_ready, 1)
            act.wait_ge(weights_loaded, 16)
            act.wait_ge(w1_lo_ready, 1)
            place_dense(0)
            for c in range(CHUNKS):
                run_chunk(c)
            read_outputs(CHUNKS - 1)

        @block.tensor
        def _(pe):
            def take_bank(n):
                if n >= BANKS:
                    pe.wait_ge(bank_read, n - BANKS + 1)
                return bank_ps[:, n % BANKS]

            def select(use):
                kind, c, t = use
                n = CANDIDATE_USE[use]
                if n >= 2:
                    pe.wait_ge(candidates_read, n - 1)
                made = sum(1 + (CHUNK_SELECTED[x] > 0) for x in range(c)) + (1 if kind == "small" else 2)
                pe.wait_ge(hot_ready, made)
                tables_split = CHUNK_SELECTED[c] if kind == "middle" else 0
                pe.wait_ge(split_steps, SMALL_SPLIT_STEPS + MIDDLE_SPLIT_STEPS * tables_split)
                bank = cand_ps[:, n % 2]
                lanes = slice(t * P, (t + 1) * P)
                if kind == "small":
                    for g in range(S_GROUPS):
                        if g < A_GROUPS:
                            at, pitch, length, n_groups, first = 0, A_COLS, LA, A_GROUPS, g
                        else:
                            at, pitch, length, n_groups, first = 2 * A_COLS, B_COLS, LB, B_GROUPS, g - A_GROUPS
                        to = bank[:, at:at + 2 * pitch].rearrange("p (l h g) -> p g h l", h=2, g=n_groups)[:, first]
                        for r in range(3):
                            by = small_parts[:, r, at:at + 2 * pitch].rearrange("p (h c) -> p h c", h=2)[
                                :, :, first * length:(first + 1) * length]
                            last = nc.tensor.matmul(to, small_hot[:, c % 2, g, lanes], by, start=r == 0, stop=r == 2)
                else:
                    for m in range(CHUNK_SELECTED[c]):
                        for r in range(3):
                            last = nc.tensor.matmul(bank[:, m * LM:(m + 1) * LM], middle_hot[:, c % 2, m, lanes],
                                                    middle_parts[:, r, m * LM:(m + 1) * LM], start=r == 0, stop=r == 2)
                last.then_inc(candidates_ready, 1)

            def layer3(c):
                n = CHUNK_TILES[c] * P
                if c:
                    pe.wait_ge(y_read, c)
                for k in range(K3):
                    pe.wait_ge(bank_read, BANK_USE["l2", c, k] + 1)
                    last = nc.tensor.matmul(y_ps[:, 0:n], w3[:, k:k + 1], h2[:, k, 0:n], start=k == 0, stop=k == K3 - 1)
                last.then_inc(y_filled, 1)

            def run_chunk(c):
                nt = CHUNK_TILES[c]
                cols = nt * P
                between = _small(c + 1) + _middle(c + 1) if c + 1 < CHUNKS else []
                steps = K2 + 1
                late = (c + 1, "between small picks") in MIDDLE_SUMS

                def fill(step):
                    first, end = ((len(between) * s + (0 if late else steps // 2)) // steps for s in (step, step + 1))
                    for use in between[first:end]:
                        select(use)

                pe.wait_ge(z_ready, 2 * c + 2)
                pe.wait_ge(dense_placed, c + 1)
                for k in range(K1):
                    n = c * K1 + k
                    if n >= 2:
                        pe.wait_ge(zt_lo_ready, n - 1)
                    for t in range(nt):
                        last = nc.tensor.transpose(zt_ps[:, n % 2, t * P:(t + 1) * P],
                                                   z[:, c % 2, t, k * P:(k + 1) * P], identity)
                    last.then_inc(z_transposed, 1)
                    if k == 1 and c:
                        layer3(c - 1)
                fill(0)
                if c == 0:
                    pe.wait_ge(w1_lo_ready, 1)
                for m in range(K2):
                    bank = take_bank(BANK_USE["l1", c, m])[:, 0:cols]
                    for k in range(K1):
                        if m == 0:
                            pe.wait_ge(zt_lo_ready, c * K1 + k + 1)
                        w_hi, w_lo = (w[:, k, m * P:(m + 1) * P] for w in (w1_hi, w1_lo))
                        z_hi, z_lo = zt_hi[:, k, 0:cols], zt_lo[:, k, 0:cols]
                        nc.tensor.matmul(bank, w_hi, z_hi, start=k == 0, stop=False)
                        nc.tensor.matmul(bank, w_hi, z_lo, start=False, stop=False)
                        last = nc.tensor.matmul(bank, w_lo, z_hi, start=False, stop=k == K1 - 1)
                    last.then_inc(bank_filled, 1)
                    fill(m + 1)
                banks = [take_bank(BANK_USE["l2", c, m])[:, 0:cols] for m in range(K3)]
                for k in range(K2):
                    if c in SPLIT_LAYER2:
                        pe.wait_ge(w2_lo_ready, 1)
                        pe.wait_ge(h1_lo_ready, h1_parts_before(c) + k + 1)
                        products = [(w2_hi, h1_hi), (w2_hi, h1_lo), (w2_lo, h1_hi)]
                    else:
                        pe.wait_ge(bank_read, BANK_USE["l1", c, k] + 1)
                        products = [(w2, h1)]
                    for m in range(K3):
                        for n, (w, h) in enumerate(products):
                            last = nc.tensor.matmul(
                                banks[m], w[:, k, m * P:(m + 1) * P], h[:, k, 0:cols],
                                start=k == 0 and n == 0, stop=k == K2 - 1 and n == len(products) - 1)
                        if k == K2 - 1:
                            last.then_inc(bank_filled, 1)

            for use in _small(0) + _middle(0):
                select(use)
            pe.wait_ge(weights_loaded, 16)
            for c in range(CHUNKS):
                run_chunk(c)
            layer3(CHUNKS - 1)


def kernel(**inputs):
    import numpy as _np
    import concourse.bacc as _bacc
    from concourse import mybir as _mybir
    from concourse.bass_utils import run_bass_kernel_spmd as _run

    nc = _bacc.Bacc("TRN2", target_bir_lowering=False, num_devices=1)
    arrays = {}

    def put(name, a):
        arrays[name] = a = _np.ascontiguousarray(a)
        return nc.dram_tensor(name, a.shape, _mybir.dt.from_np(a.dtype), kind="ExternalInput").ap()

    tables = [_np.asarray(inputs[f"tbl_{f}"]) for f in SLOTS]

    def streamed(slots, halves, lanes, length):
        groups = len(slots) // halves
        a = _np.zeros((halves, groups, lanes * length, EMBED), _np.float32)
        for n, slot in enumerate(slots):
            if slot is not None:
                a[n // groups, n % groups, :len(tables[slot])] = tables[slot]
        a = a.reshape(halves, groups, lanes, length, EMBED).transpose(0, 2, 1, 3, 4)
        return a.reshape(halves * lanes, groups * length, EMBED)

    def by_half_rows(a):
        return a.reshape(P, -1, 2, HALF_ROW).transpose(2, 0, 1, 3).reshape(2, P, -1)

    row_of = {}
    for i in range(FIELDS - 1):
        for j in range(i + 1, FIELDS):
            row_of[i, j] = row_of[j, i] = len(row_of) // 2
    order = [row_of[SLOTS[i], SLOTS[j]] for i, j in pair_order()] + list(range(PAIRS, PAIRS + DENSE))

    def by_tile(a):
        return a.reshape(TILES, P, -1).transpose(1, 0, 2)

    def by_partition(w):
        w = _np.asarray(w).reshape(-1, P, w.shape[-1] if w.ndim > 1 else 1)
        return w.transpose(1, 0, 2).reshape(P, -1)

    weights = _np.concatenate(
        [by_partition(inputs[n]) for n in ("W_top2", "W_top3", "b_top1", "b_top2")]
        + [_np.eye(P, dtype=_np.float32)], axis=1)

    multipliers = _np.zeros((len(BY_HALF), 1), _np.float32)
    for n, slot in enumerate(BY_HALF):
        if slot is not None:
            multipliers[n, 0] = MULTIPLIER[LA if slot < A_SLOTS else LB if slot < SMALL else LM]

    ids = _np.asarray(inputs["ids"])[:, SLOTS]
    by_slot = _np.zeros((len(BY_HALF), TILES, P), ids.dtype)
    for n, slot in enumerate(BY_HALF):
        if slot is not None:
            by_slot[n] = ids[:, slot].reshape(TILES, P)
    gathered_tables = [put(f"table_{s}", tables[s]) if s >= SMALL + min(CHUNK_SELECTED) else None
                       for s in range(FIELDS)]
    build_program(
        nc, put("ids", by_tile(ids)), put("ids_by_slot", by_slot.reshape(-1, BATCH)),
        put("dense_ctx", by_tile(_np.asarray(inputs["dense_ctx"]))),
        put("w1", by_partition(_np.asarray(inputs["W_top1"])[order])), put("weights", weights),
        put("multipliers", multipliers),
        put("rows_a", streamed(list(range(A_SLOTS)), 2, 64, LA).reshape(P, -1)),
        put("rows_b", streamed(list(range(A_SLOTS, SMALL)) + [None], 2, 64, LB).reshape(P, -1)),
        [put(f"rows_m{m}", by_half_rows(streamed([SMALL + m], 1, P, LM))) for m in range(M_SEL)],
        gathered_tables,
        nc.dram_tensor("hi_by_slot", (len(BY_HALF), BATCH), _mybir.dt.bfloat16, kind="Internal").ap(),
        nc.dram_tensor("out", (BATCH, 1), _mybir.dt.float32, kind="ExternalOutput").ap())
    r = _run(nc, [arrays], core_ids=[0])
    return r.results[0]["out"]
```
